# Optimizing a Trainium2 kernel written in Bass

```python
import numpy as np
import jax
import jax.numpy as jnp

def _softmax(x, axis=-1):
    return jax.nn.softmax(x, axis=axis)

def _gelu(x):
    return jax.nn.gelu(x, approximate=True)

def _silu(x):
    return jax.nn.silu(x)

def _sigmoid(x):
    return jax.nn.sigmoid(x)

def _layernorm(x, axis=-1, eps=1e-05):
    m = jnp.mean(x, axis=axis, keepdims=True)
    v = jnp.var(x, axis=axis, keepdims=True)
    return (x - m) / jnp.sqrt(v + eps)

def _scatter_add(tgt, idx, src, axis=0):
    return tgt.at[idx].add(src)

def _segment_sum(src, seg, n):
    return jax.ops.segment_sum(src, seg, n)
kernel_name = 'mk_flamingo_gated_d1_seqx_r8_118798'

def setup_inputs(seed: int=0):
    np.random.seed(seed)
    _w = jnp.asarray

    def _rec_inputs():
        import jax
        import jax.numpy as jnp
        _rk = jax.random.key(seed)
        x = -0.0002928 + 1 * jax.random.normal(jax.random.fold_in(_rk, 1), (16, 128, 256), jnp.float32)
        _lenS = 128 - jax.random.randint(jax.random.fold_in(_rk, 7), (16,), 0, max(1, 128 // 4) + 1, jnp.int32)
        _lenS2 = 128 - jax.random.randint(jax.random.fold_in(_rk, 8), (16,), 0, max(1, 128 // 4) + 1, jnp.int32)
        _ctx_2048P = jax.random.normal(jax.random.fold_in(_rk, 11), (16, 16, 256), jnp.float32)
        _ctx_2048c = jax.random.dirichlet(jax.random.fold_in(_rk, 511), 0.3 * jnp.ones((16,), jnp.float32), (16, 128))
        _ctx_2048t = jnp.einsum('bsk,bkd->bsd', _ctx_2048c, _ctx_2048P)
        _ctx_2048t = _ctx_2048t * jax.lax.rsqrt(jnp.mean(jnp.square(_ctx_2048t)) + 1e-12) * 0.953939
        ctx_2048 = -1.39393e-06 + 0.999914 * (_ctx_2048t + 0.3 * jax.random.normal(jax.random.fold_in(_rk, 611), (16, 128, 256), jnp.float32))
        _g = jax.random.normal(jax.random.fold_in(_rk, 9001), (2, 1), jnp.float32)
        _g = jnp.sign(_g) * jnp.maximum(jnp.abs(_g), 1.0) + (_g == 0) * 1.0
        g_xattn = _g[0]
        g_ffn = _g[1]
        return (x, ctx_2048, g_xattn, g_ffn)
    x, ctx_2048, g_xattn, g_ffn = _rec_inputs()

    def _L0_xattn_setup():
        import jax, jax.numpy as jnp
        import numpy as np
        HID = 256
        H = 32
        HK = 8
        G = H // HK
        D = HID // H
        T = 128
        W_ATT = 32
        W_SSM = 64

        def _heads(x, n):
            B, Tt, _ = x.shape
            return x.reshape(B, Tt, n, D).transpose(0, 2, 1, 3)

        def _attend(q, k, v):
            pos = jnp.arange(T)
            rel = pos[None, :] - pos[:, None]
            slopes = jnp.power(2.0, -8.0 * jnp.arange(H, dtype=jnp.float32) / H)
            alibi = slopes[:, None, None] * rel.astype(jnp.float32)
            bias = jnp.concatenate([alibi, alibi], axis=-1)
            delta = -rel
            ssm_mask = (delta >= 0) & (delta < W_SSM)
            att_mask = (delta >= 0) & (delta < W_ATT)
            mask = jnp.concatenate([ssm_mask, att_mask], axis=-1)
            scores = jnp.einsum('bhqd,bhkd->bhqk', q, k) / np.sqrt(D).astype(np.float32)
            scores = scores + bias[None]
            scores = jnp.where(mask[None, None], scores, -jnp.inf)
            wei = jax.nn.softmax(scores, axis=-1)
            return jnp.einsum('bhqk,bhkd->bhqd', wei, v)
        key = jax.random.key(seed)
        ks = jax.random.split(key, 8)
        s = lambda fan_in: 1.0 / np.sqrt(fan_in)
        return {'hidden_states': jax.random.normal(ks[0], (2, T, HID), jnp.float32), 'ssm_states': jax.random.normal(ks[1], (2, T, HID), jnp.float32), 'Wq': jax.random.normal(ks[2], (2 * HID, HID), jnp.float32) * s(2 * HID), 'Wk': jax.random.normal(ks[3], (HID, HK * D), jnp.float32) * s(HID), 'Wv': jax.random.normal(ks[4], (HID, HK * D), jnp.float32) * s(HID), 'Wsk': jax.random.normal(ks[5], (HID, HK * D), jnp.float32) * s(HID), 'Wsv': jax.random.normal(ks[6], (HID, HK * D), jnp.float32) * s(HID), 'Wo': jax.random.normal(ks[7], (HID, HID), jnp.float32) * s(HID)}
    _L0_xattn_all = _L0_xattn_setup()
    _L0_xattn_in = {k: v for k, v in _L0_xattn_all.items() if k in ('Wq', 'Wk', 'Wv', 'Wsk', 'Wsv', 'Wo')}
    del _L0_xattn_all

    def _L0_ffn_setup():
        import jax, jax.numpy as jnp
        import numpy as np
        B, T, D = (2, 128, 256)
        H, K, DK = (4, 8, 64)
        E = 2048
        NK = 128
        key = jax.random.key(seed)
        k1, k2, k3, k4, k5 = jax.random.split(key, 5)
        x = jax.random.normal(k1, (B, T, D), dtype=jnp.float32)
        Wq = jax.random.normal(k2, (D, 2 * H * DK), dtype=jnp.float32) * 0.02
        keys = jax.random.normal(k3, (H, NK, 2, DK), dtype=jnp.float32) * 0.02
        e_down = jax.random.normal(k4, (E, D), dtype=jnp.float32) * 0.01
        e_up = jax.random.normal(k5, (E, D), dtype=jnp.float32) * 0.01
        return {'x': x, 'Wq': Wq, 'keys': keys, 'e_down': e_down, 'e_up': e_up}
    _L0_ffn_all = _L0_ffn_setup()
    _L0_ffn_in = {k: v for k, v in _L0_ffn_all.items() if k in ('Wq', 'keys', 'e_down', 'e_up')}
    del _L0_ffn_all
    return {'x': x, 'ctx_2048': ctx_2048, 'g_xattn': g_xattn, 'g_ffn': g_ffn, 'L0_xattn_Wq': _L0_xattn_in['Wq'], 'L0_xattn_Wk': _L0_xattn_in['Wk'], 'L0_xattn_Wv': _L0_xattn_in['Wv'], 'L0_xattn_Wsk': _L0_xattn_in['Wsk'], 'L0_xattn_Wsv': _L0_xattn_in['Wsv'], 'L0_xattn_Wo': _L0_xattn_in['Wo'], 'L0_ffn_Wq': _L0_ffn_in['Wq'], 'L0_ffn_keys': _L0_ffn_in['keys'], 'L0_ffn_e_down': _L0_ffn_in['e_down'], 'L0_ffn_e_up': _L0_ffn_in['e_up']}

def reference(x, ctx_2048, g_xattn, g_ffn, L0_xattn_Wq, L0_xattn_Wk, L0_xattn_Wv, L0_xattn_Wsk, L0_xattn_Wsv, L0_xattn_Wo, L0_ffn_Wq, L0_ffn_keys, L0_ffn_e_down, L0_ffn_e_up):
    import jax
    import jax.numpy as jnp

    def _L0_xattn_ref(hidden_states, ssm_states, Wq, Wk, Wv, Wsk, Wsv, Wo):
        import jax, jax.numpy as jnp
        import numpy as np
        HID = 256
        H = 32
        HK = 8
        G = H // HK
        D = HID // H
        T = 128
        W_ATT = 32
        W_SSM = 64

        def _heads(x, n):
            B, Tt, _ = x.shape
            return x.reshape(B, Tt, n, D).transpose(0, 2, 1, 3)

        def _attend(q, k, v):
            pos = jnp.arange(T)
            rel = pos[None, :] - pos[:, None]
            slopes = jnp.power(2.0, -8.0 * jnp.arange(H, dtype=jnp.float32) / H)
            alibi = slopes[:, None, None] * rel.astype(jnp.float32)
            bias = jnp.concatenate([alibi, alibi], axis=-1)
            delta = -rel
            ssm_mask = (delta >= 0) & (delta < W_SSM)
            att_mask = (delta >= 0) & (delta < W_ATT)
            mask = jnp.concatenate([ssm_mask, att_mask], axis=-1)
            scores = jnp.einsum('bhqd,bhkd->bhqk', q, k) / np.sqrt(D).astype(np.float32)
            scores = scores + bias[None]
            scores = jnp.where(mask[None, None], scores, -jnp.inf)
            wei = jax.nn.softmax(scores, axis=-1)
            return jnp.einsum('bhqk,bhkd->bhqd', wei, v)
        B = hidden_states.shape[0]
        q = _heads(jnp.concatenate([ssm_states, hidden_states], axis=-1) @ Wq, H)
        k = _heads(hidden_states @ Wk, HK)
        v = _heads(hidden_states @ Wv, HK)
        ssm_k = _heads(ssm_states @ Wsk, HK)
        ssm_v = _heads(ssm_states @ Wsv, HK)
        rep = lambda x: jnp.repeat(x, G, axis=1)
        kcat = jnp.concatenate([rep(ssm_k), rep(k)], axis=2)
        vcat = jnp.concatenate([rep(ssm_v), rep(v)], axis=2)
        o = _attend(q, kcat, vcat)
        o = o.transpose(0, 2, 1, 3).reshape(B, T, HID)
        return o @ Wo

    def _L0_ffn_ref(x, Wq, keys, e_down, e_up):
        import jax, jax.numpy as jnp
        import numpy as np
        B, T, D = (2, 128, 256)
        H, K, DK = (4, 8, 64)
        E = 2048
        NK = 128
        b, t, d = x.shape
        q = (x @ Wq).reshape(b, t, H, 2, DK)
        q1, q2 = (q[..., 0, :], q[..., 1, :])
        sim1 = jnp.einsum('bthd,hkd->bthk', q1, keys[:, :, 0, :])
        sim2 = jnp.einsum('bthd,hkd->bthk', q2, keys[:, :, 1, :])
        s1, i1 = jax.lax.top_k(sim1, K)
        s2, i2 = jax.lax.top_k(sim2, K)
        all_scores = (s1[..., :, None] + s2[..., None, :]).reshape(b, t, H, K * K)
        all_indices = (i1[..., :, None] * NK + i2[..., None, :]).reshape(b, t, H, K * K)
        final_scores, pk_idx = jax.lax.top_k(all_scores, K)
        final_indices = jnp.take_along_axis(all_indices, pk_idx, axis=-1)
        w_down = e_down[final_indices]
        w_up = e_up[final_indices]
        hidden = jnp.einsum('btd,bthkd->bthk', x, w_down)
        hidden = jax.nn.silu(hidden)
        hidden = hidden * jax.nn.relu(final_scores)
        out = jnp.einsum('bthk,bthkd->btd', hidden, w_up)
        return out
    x = x + jnp.tanh(g_xattn[0]) * _L0_xattn_ref(_layernorm(x, axis=-1), ctx_2048, L0_xattn_Wq, L0_xattn_Wk, L0_xattn_Wv, L0_xattn_Wsk, L0_xattn_Wsv, L0_xattn_Wo)
    x = x + jnp.tanh(g_ffn[0]) * _L0_ffn_ref(_layernorm(x, axis=-1), L0_ffn_Wq, L0_ffn_keys, L0_ffn_e_down, L0_ffn_e_up)
    return x

_drawn_inputs = setup_inputs


def setup_inputs(seed=0):
    import zlib

    import numpy as np

    out = dict(_drawn_inputs(seed))
    spreads = {}
    factors = {'L0_ffn_Wq': 8.0, 'L0_ffn_keys': 8.0, 'L0_ffn_e_down': 8.0, 'L0_ffn_e_up': 8.0}
    for name, (base, spread) in spreads.items():
        noise = np.random.default_rng([zlib.crc32(name.encode()), seed]).standard_normal(out[name].shape)
        drawn = base * np.exp(spread * noise) if base else spread * noise
        out[name] = jnp.asarray(drawn.astype(out[name].dtype))
    for name, factor in factors.items():
        out[name] = (out[name] * factor).astype(out[name].dtype)
    return out
```

```python
from contextlib import ExitStack

import numpy as np

import concourse.bass as bass
from concourse import mybir

F32 = mybir.dt.float32
BF16 = mybir.dt.bfloat16
U32 = mybir.dt.uint32
ALU = mybir.AluOpType
ACT = mybir.ActivationFunctionType
AX_X = mybir.AxisListType.X

B, T, HID = 16, 128, 256
KC = HID // 128
NH, NKV, D = 32, 8, 8
NP = NH // 2
W_SSM, W_ATT = 64, 32
QB = 64
K1, K2, K3 = 128, 128, 96
KALL = K1 + K2 + K3
A3_LO = T - K3
Q_PART = [0, 0, 0, 1, 1, 2]
K_RUNS = [(0, 3), (3, 2), (5, 1)]
R_QK = len(Q_PART) * D
R_ALIBI, N_ALIBI = R_QK, 3
R_MASK = R_ALIBI + N_ALIBI
R_MAX, N_MAX = R_MASK + QB, 2
ROWS = R_MAX + N_MAX
MASKED = -1e30
FH, FK, DK, NK, E = 4, 8, 64, 128, 2048
NI1 = E // NK
NPICK = FH * FK
NG = T // 4
EPS = 1e-5

STORES = 5 * 16
QK_DMAS = (len(Q_PART) + len(K_RUNS)) * 16
M_DMAS = N_MAX * 16
NFILL = 12


def program(nc, x, ctx_t, g, wq, wk, wv, wsk, wsv, wo, fwq, keys_t, down_t, up,
            c_ident, c_krows, c_qrows, c_iota2, c_iota1, c_ranks, out):
    st = ExitStack()
    with st:
        def sb(name, shape, dt=F32):
            return st.enter_context(nc.sbuf_tensor(name, shape, dt))

        def ps(name):
            return st.enter_context(nc.psum_tensor(name, [128, 512], F32))

        def sem(name):
            return st.enter_context(nc.semaphore(name))

        wq_sb = sb("wq_sb", [128, 2 * KC, HID])
        wk_sb = sb("wk_sb", [128, 2, KC, NKV * D])
        wv_sb = sb("wv_sb", [128, 2, KC, NKV * D])
        wo_sb = sb("wo_sb", [128, 2, HID])
        fwq_sb = sb("fwq_sb", [128, KC, 2 * FH * DK])
        keys_sb = sb("keys_sb", [128, FH, NK])
        down_sb = sb("down_sb", [128, KC, E])
        up_sb = sb("up_sb", [128, NI1, HID])
        ident = sb("ident", [128, 128])
        iota2 = sb("iota2", [128, NK, NG], BF16)
        iota1 = sb("iota1", [128, 4, NI1, NG], BF16)
        ranks = sb("ranks", [128, FK])
        gates = sb("gates", [128, 2])
        half_neg = sb("half_neg", [128, 1])

        x_in = sb("x_in", [128, HID])
        x_res = sb("x_res", [128, HID])
        ctx_sb = sb("ctx_sb", [128, KC, T])
        stats = sb("stats", [128, 6])
        mv = sb("mv", [128, 2])
        var_eps = sb("var_eps", [128, 1])
        rstd = sb("rstd", [128, 1])
        xn = sb("xn", [128, HID])
        xn_t = sb("xn_t", [128, KC, T])
        qk_parts = sb("qk_parts", [128, 3, 3 * T], BF16)
        qk_rest = sb("qk_rest", [128, 3 * T])
        q_op = sb("q_op", [ROWS, NP, 2, 2 * QB], BF16)
        k_op = sb("k_op", [ROWS, NKV, KALL], BF16)
        v_sb = sb("v_sb", [128, 3, NKV, D + 1])
        m_neg = sb("m_neg", [128, NP, 2])
        mt_parts = sb("mt_parts", [2 * NP, N_MAX, 128], BF16)
        probs = sb("probs", [128, 2, 3, 512])
        rden = sb("rden", [128, 2 * NP])
        o_norm = sb("o_norm", [128, 2 * NP, D])
        o_t = sb("o_t", [128, 2, T])
        x2 = sb("x2", [128, HID])
        x2_last = sb("x2_last", [128, HID])

        stats2 = sb("stats2", [128, 6])
        mv2 = sb("mv2", [128, 2])
        var_eps2 = sb("var_eps2", [128, 1])
        rstd2 = sb("rstd2", [128, 1])
        xn2 = sb("xn2", [128, HID])
        xn2_t = sb("xn2_t", [128, KC, T])
        fq_t = sb("fq_t", [128, FH, T])
        sims = sb("sims", [128, 2, FH, NK])
        top_s = sb("top_s", [128, 2, FH, FK])
        top_i = sb("top_i", [128, 2, FH, FK], U32)
        top_if = sb("top_if", [128, 2 * FH, FK])
        pair_s = sb("pair_s", [128, FH, FK, FK])
        fin_s = sb("fin_s", [128, FH, FK])
        fin_i = sb("fin_i", [128, NPICK], U32)
        rank12 = sb("rank12", [128, 2, NPICK], U32)
        hot_r = sb("hot_r", [128, 2 * NPICK, FK])
        val_r = sb("val_r", [128, 2 * NPICK, FK])
        pick_i = sb("pick_i", [128, 2, NPICK])
        beyond = sb("beyond", [128, NPICK])
        picks = sb("picks", [128, 3, NPICK])
        picks_t = sb("picks_t", [128, 3, NG])
        ib = sb("ib", [128, 2, NG], BF16)
        w_parts = sb("w_parts", [128, 3, NG], BF16)
        w_rest = sb("w_rest", [128, NG])
        hot2 = sb("hot2", [128, NK, NG], BF16)
        hot1 = sb("hot1", [128, 4 * NI1, NG], BF16)
        w_hot1 = sb("w_hot1", [128, 3, 4 * NI1, NG], BF16)
        hs = sb("hs", [128, NI1, T])
        act_t = sb("act_t", [128, NI1, T])
        y = sb("y", [128, HID])

        q_scratch = nc.dram_tensor("q_scratch", (3, D, NP, 2 * T), BF16, kind="Internal").ap()
        k_scratch = nc.dram_tensor("k_scratch", (3, D, NKV, KALL), BF16, kind="Internal").ap()

        score_ps = [ps("score_ps0"), ps("score_ps1")]
        o_ps = ps("o_ps")
        att_ps = ps("att_ps")
        h_ps = [ps("h_ps0"), ps("h_ps1")]
        c_ps = ps("c_ps")
        ffn_ps = ps("ffn_ps")
        coef_ps = [c_ps, h_ps[0], h_ps[1], c_ps]

        att_w_loaded = sem("att_w_loaded")
        ffn_w_loaded = sem("ffn_w_loaded")
        up_loaded = sem("up_loaded")
        x_loaded = sem("x_loaded")
        ctx_loaded = sem("ctx_loaded")
        res_loaded = sem("res_loaded")
        parts_stored = sem("parts_stored")
        operands_loaded = sem("operands_loaded")
        max_loaded = sem("max_loaded")
        out_stored = sem("out_stored")
        setup_done = sem("setup_done")
        wq_scaled = sem("wq_scaled")
        gates_ready = sem("gates_ready")
        var_ready = sem("var_ready")
        rstd_ready = sem("rstd_ready")
        xn_ready = sem("xn_ready")
        xn_transposed = sem("xn_transposed")
        xn_t_ready = sem("xn_t_ready")
        qk_projected = sem("qk_projected")
        v_projected = sem("v_projected")
        v_ready = sem("v_ready")
        first_v_ready = sem("first_v_ready")
        hi_ready = sem("hi_ready")
        rest_ready = sem("rest_ready")
        mid_ready = sem("mid_ready")
        parts_ready = sem("parts_ready")
        max_filled = sem("max_filled")
        max_taken = sem("max_taken")
        max_transposed = sem("max_transposed")
        max_split = sem("max_split")
        scores_filled = sem("scores_filled")
        exp_done = sem("exp_done")
        pv_done = sem("pv_done")
        o_normed = sem("o_normed")
        o_transposed = sem("o_transposed")
        o_t_ready = sem("o_t_ready")
        wo_done = sem("wo_done")
        x2_ready = sem("x2_ready")
        var2_ready = sem("var2_ready")
        rstd2_ready = sem("rstd2_ready")
        xn2_ready = sem("xn2_ready")
        xn2_transposed = sem("xn2_transposed")
        xn2_t_ready = sem("xn2_t_ready")
        fq_projected = sem("fq_projected")
        fq_t_ready = sem("fq_t_ready")
        sims_filled = sem("sims_filled")
        sims_ready = sem("sims_ready")
        hot2_ready = sem("hot2_ready")
        hot1_ready = sem("hot1_ready")
        h_filled = sem("h_filled")
        hs_ready = sem("hs_ready")
        coef_filled = sem("coef_filled")
        act_ready = sem("act_ready")
        up_done = sem("up_done")
        y_ready = sem("y_ready")
        dve_step = sem("dve_step")

        block = st.enter_context(nc.Block())

        @block.sync
        def _(sp):
            def load(dst, src, s):
                sp.dma_start(dst, src).then_inc(s, 16)

            load(x_in[:, :], x[0, :, :], x_loaded)
            load(ctx_sb[:, :, :], ctx_t[0, :, :, :], ctx_loaded)
            load(ident[:, :], c_ident[:, :], att_w_loaded)
            load(wq_sb[:, :, :], wq.rearrange("(k p) n -> p k n", p=128), att_w_loaded)
            for a, (kk, vv) in enumerate(((wsk, wsv), (wk, wv))):
                load(wk_sb[:, a], kk.rearrange("(k p) n -> p k n", p=128), att_w_loaded)
                load(wv_sb[:, a], vv.rearrange("(k p) n -> p k n", p=128), att_w_loaded)
            load(k_op[R_ALIBI:ROWS, :, :], c_krows[:, :, :], att_w_loaded)
            load(q_op[R_ALIBI:R_MAX, :, :, :], c_qrows[:, :, :, :], att_w_loaded)
            load(wo_sb[:, :, :], wo[:, :, :], att_w_loaded)
            load(gates[:, :], g[:, :], att_w_loaded)

            def operands(i):
                sp.wait_ge(parts_ready, i + 1)
                load(q_scratch.rearrange("a d n t -> (d n) a t"), qk_parts[:, :, 0:2 * T], parts_stored)
                for a, lo, n, at in ((0, 0, QB, 0), (1, 0, QB, QB), (0, 0, T, K1), (1, A3_LO, K3, K1 + K2)):
                    load(k_scratch[:, :, :, at:at + n].rearrange("a d n t -> (d n) a t"),
                         qk_parts[64 * a:64 * a + 64, :, 2 * T + lo:2 * T + lo + n], parts_stored)
                sp.wait_ge(parts_stored, STORES * (i + 1))
                for r, pq in enumerate(Q_PART):
                    load(q_op[D * r:D * r + D, :, :, :].rearrange("r p b t -> r (p b t)"),
                         q_scratch[pq].rearrange("d n t -> d (n t)"), operands_loaded)
                for r, n in K_RUNS:
                    load(k_op[D * r:D * (r + n), :, :].rearrange("r n t -> r (n t)"),
                         k_scratch[0:n].rearrange("a d n t -> (a d) (n t)"), operands_loaded)

            def prefetch(i):
                sp.wait_ge(xn_ready, i)
                load(x_in[:, :], x[i, :, :], x_loaded)
                sp.wait_ge(v_projected, i)
                load(ctx_sb[:, :, :], ctx_t[i, :, :, :], ctx_loaded)

            def residual(i):
                sp.wait_ge(x2_ready, i)
                load(x_res[:, :], x[i, :, :], res_loaded)

            def maxima(i):
                sp.wait_ge(max_split, i + 1)
                for part in range(N_MAX):
                    row = R_MAX + part
                    load(q_op[row:row + 1, :, :, :].rearrange("r p b t -> r (p b) t"), mt_parts[:, part, :], max_loaded)

            def store(j):
                sp.wait_ge(y_ready, j + 1)
                sp.dma_start(out[j, :, :], y[:, :]).then_inc(out_stored, 16)
                sp.wait_ge(out_stored, 16 * j + 16)

            operands(0)
            load(fwq_sb[:, :, :], fwq.rearrange("(k p) n -> p k n", p=128), ffn_w_loaded)
            load(keys_sb[:, :, :], keys_t[:, :, :], ffn_w_loaded)
            load(ranks[:, :], c_ranks[:, :], ffn_w_loaded)
            prefetch(1)
            load(x_res[:, :], x[0, :, :], res_loaded)
            load(down_sb[:, :, :], down_t.rearrange("(k p) n -> p k n", p=128), ffn_w_loaded)
            load(iota2[:, :, :], c_iota2[:, :, :], ffn_w_loaded)
            load(iota1[:, :, :, :], c_iota1[:, :, :, :], ffn_w_loaded)
            maxima(0)
            load(up_sb[:, :, :], up.rearrange("(a p) n -> p a n", p=128), up_loaded)
            operands(1)
            residual(1)
            maxima(1)
            prefetch(2)
            with sp.Fori(2, B - 1) as i:
                operands(i)
                residual(i)
                maxima(i)
                store(i - 2)
                prefetch(i + 1)
            operands(B - 1)
            residual(B - 1)
            maxima(B - 1)
            for j in range(B - 3, B):
                store(j)

        @block.gpsimd
        def _(pool):
            pool.memset(half_neg[:, :], -0.5).then_inc(setup_done, 1)
            pool.memset(v_sb[:, :, :, D:D + 1], 1.0).then_inc(setup_done, 1)
            pool.wait_ge(setup_done, 1)

            def norm1(i):
                pool.wait_ge(var_ready, i + 1)
                pool.tensor_tensor(rstd[:, :], var_eps[:, :], half_neg[:, :], ALU.pow).then_inc(rstd_ready, 1)

            def norm2(i):
                pool.wait_ge(var2_ready, i + 1)
                pool.tensor_tensor(rstd2[:, :], var_eps2[:, :], half_neg[:, :], ALU.pow).then_inc(rstd2_ready, 1)

            norm1(0)
            with pool.Fori(1, B) as i:
                norm1(i)
                norm2(i - 1)
            norm2(B - 1)

        @block.scalar
        def _(act):
            act.wait_ge(att_w_loaded, 10 * 16)
            nc.scalar.mul(wq_sb[:, :, :], wq_sb[:, :, :], float(D) ** -0.5).then_inc(wq_scaled, 1)
            nc.scalar.activation(gates[:, :], gates[:, :], ACT.Tanh).then_inc(gates_ready, 1)
            act.wait_ge(setup_done, 2)

            def att_head(i):
                act.wait_ge(xn_transposed, i + 1)
                nc.scalar.copy(xn_t[:, :, :], att_ps[:, 0:KC * T].rearrange("p (k t) -> p k t", t=T)).then_inc(xn_t_ready, 1)

            def att_parts(i):
                act.wait_ge(qk_projected, i + 1)
                act.wait_ge(parts_stored, STORES * i)
                blocks = "p (h b q) -> p b h q"
                nc.scalar.copy(qk_parts[:, 0, 0:2 * T].rearrange("p (b h q) -> p b h q", b=2, h=2),
                               score_ps[0][:, 0:2 * T].rearrange(blocks, h=2, b=2))
                nc.scalar.copy(qk_parts[:, 0, 2 * T:3 * T], score_ps[0][:, 2 * T:3 * T]).then_inc(hi_ready, 1)
                act.wait_ge(v_projected, i + 1)
                v = score_ps[1][:, 0:3 * NKV * D].rearrange("p (n h d) -> p n h d", n=3, d=D)
                nc.scalar.copy(v_sb[:, 1, :, 0:D], v[:, 1])
                nc.scalar.copy(v_sb[0:K3, 2, :, 0:D], v[0:K3, 2]).then_inc(v_ready, 1)
                act.wait_ge(rest_ready, i + 1)
                nc.scalar.copy(qk_parts[:, 1, :], qk_rest[:, :]).then_inc(mid_ready, 1)

            def ffn_head(j):
                act.wait_ge(xn2_transposed, j + 1)
                nc.scalar.copy(xn2_t[:, :, :], ffn_ps[:, 0:KC * T].rearrange("p (k t) -> p k t", t=T)).then_inc(xn2_t_ready, 1)

            def ffn_sims(j):
                act.wait_ge(fq_projected, j + 1)
                nc.scalar.copy(fq_t[:, :, :], c_ps[:, :].rearrange("p (h t) -> p h t", t=T)).then_inc(fq_t_ready, 1)
                act.wait_ge(sims_filled, j + 1)
                for half in range(2):
                    nc.scalar.copy(sims[:, half], h_ps[half][:, :].rearrange("p (h n) -> p h n", n=NK)).then_inc(sims_ready, 1)

            def silus(j):
                for c in range(4):
                    act.wait_ge(h_filled, 4 * j + c + 1)
                    nc.scalar.activation(hs[:, 4 * c:4 * c + 4, :].rearrange("p a t -> p (a t)"), h_ps[c % 2][:, :],
                                         ACT.Silu).then_inc(hs_ready, 1)

            def exps(i):
                for c in range(4):
                    act.wait_ge(pv_done, 4 * i + c - 1 if c else 4 * i)
                    for s in range(3):
                        n = 3 * c + s
                        keys = K3 if s == 2 else 128
                        act.wait_ge(scores_filled, NFILL * i + n + 1)
                        nc.scalar.activation(probs[0:keys, c % 2, s, :], score_ps[n % 2][0:keys, :], ACT.Exp).then_inc(exp_done, 1)

            def att_tail(i):
                act.wait_ge(o_transposed, i + 1)
                src = att_ps[:, 0:2 * 128].rearrange("p (b h q) -> p h b q", b=2, h=2)
                nc.scalar.copy(o_t[:, :, :].rearrange("p h (b q) -> p h b q", b=2), src).then_inc(o_t_ready, 1)

            def batch(i, att, mid):
                if att:
                    att_head(i)
                    att_parts(i)
                if mid:
                    ffn_head(i - 1)
                    ffn_sims(i - 1)
                    silus(i - 1)
                if att:
                    exps(i)
                    att_tail(i)

            batch(0, True, False)
            with act.Fori(1, B) as i:
                batch(i, True, True)
            batch(B, False, True)

        @block.vector
        def _(dve):
            v = nc.vector
            steps = {"n": 0}

            def link(ins):
                steps["n"] += 1
                ins.then_inc(dve_step, 1)
                dve.wait_ge(dve_step, steps["n"])

            def restart():
                dve.sem_clear(dve_step)
                steps["n"] = 0

            def norm_stats(src, stats, mv, var_eps, var_sem):
                link(v.bn_stats(stats[:, :], src[:, :]))
                link(v.bn_aggr(mv[:, :], stats[:, :]))
                v.tensor_scalar_add(var_eps[:, :], mv[:, 1:2], EPS).then_inc(var_sem, 1)

            def norm_apply(src, mv, rstd, xn, sem):
                v.tensor_scalar(xn[:, :], src[:, :], mv[:, 0:1], rstd[:, 0:1], ALU.subtract, ALU.mult).then_inc(sem, 1)

            def att_parts(i):
                dve.wait_ge(hi_ready, i + 1)
                blocks, put = "p (h b q) -> p b h q", "p (b h q) -> p b h q"
                v.tensor_tensor(qk_rest[:, 0:2 * T].rearrange(put, b=2, h=2), score_ps[0][:, 0:2 * T].rearrange(blocks, h=2, b=2),
                                qk_parts[:, 0, 0:2 * T].rearrange(put, b=2, h=2), ALU.subtract)
                v.tensor_tensor(qk_rest[:, 2 * T:3 * T], score_ps[0][:, 2 * T:3 * T], qk_parts[:, 0, 2 * T:3 * T],
                                ALU.subtract).then_inc(rest_ready, 1)
                dve.wait_ge(mid_ready, i + 1)
                v.tensor_tensor(qk_parts[:, 2, :], qk_rest[:, :], qk_parts[:, 1, :], ALU.subtract).then_inc(parts_ready, 1)

            def first_v(upper):
                r = slice(64 * upper, 64 * upper + 64)
                src = score_ps[1][r, (1 - upper) * NKV * D:(2 - upper) * NKV * D]
                v.tensor_copy(v_sb[r, 0, :, 0:D], src.rearrange("p (h d) -> p h d", d=D)).then_inc(first_v_ready, 1)

            def top(j, att):
                for half in range(2):
                    dve.wait_ge(sims_ready, 2 * j + half + 1)
                    if att:
                        first_v(half)
                    for h in range(FH):
                        last = v.max(top_s[:, half, h], sims[:, half, h])
                link(last)
                for half in range(2):
                    for h in range(FH):
                        last = v.max_index(top_i[:, half, h], top_s[:, half, h], sims[:, half, h])
                link(v.tensor_tensor(pair_s[:, :, :, :], top_s[:, 0].unsqueeze(3).broadcast_to([128, FH, FK, FK]),
                                     top_s[:, 1].unsqueeze(2).broadcast_to([128, FH, FK, FK]), ALU.add))
                v.tensor_copy(top_if[:, :, :], top_i[:, :, :, :].rearrange("p a h k -> p (a h) k"))
                for h in range(FH):
                    last = v.max(fin_s[:, h], pair_s[:, h].rearrange("p a b -> p (a b)"))
                link(last)
                for h in range(FH):
                    last = v.max_index(fin_i[:, h * FK:(h + 1) * FK], fin_s[:, h], pair_s[:, h].rearrange("p a b -> p (a b)"))
                link(last)
                v.tensor_scalar(rank12[:, 0, :], fin_i[:, :], 3, None, ALU.logical_shift_right)
                link(v.tensor_scalar(rank12[:, 1, :], fin_i[:, :], FK - 1, None, ALU.bitwise_and))
                link(v.tensor_tensor(hot_r[:, :, :],
                                     rank12[:, :, :].rearrange("p a n -> p (a n)").unsqueeze(2).broadcast_to([128, 2 * NPICK, FK]),
                                     ranks[:, :].unsqueeze(1).broadcast_to([128, 2 * NPICK, FK]), ALU.is_equal))
                link(v.tensor_tensor(val_r[:, :, :].rearrange("p (a k) r -> p a k r", k=FK),
                                     hot_r[:, :, :].rearrange("p (a k) r -> p a k r", k=FK),
                                     top_if[:, :, :].unsqueeze(2).broadcast_to([128, 2 * FH, FK, FK]), ALU.mult))
                link(v.tensor_reduce(pick_i[:, :, :].rearrange("p a n -> p (a n)"), val_r[:, :, :], AX_X, ALU.add))
                v.tensor_scalar(beyond[:, :], pick_i[:, 0, :], float(NI1), float(NK - 1), ALU.is_ge, ALU.mult)
                v.tensor_scalar(picks[:, 0, :], pick_i[:, 0, :], float(NI1 - 1), None, ALU.min)
                link(v.tensor_scalar(picks[:, 2, :], fin_s[:, :, :].rearrange("p h k -> p (h k)"), 0.0, None, ALU.max))
                link(v.tensor_tensor(picks[:, 1, :], pick_i[:, 1, :], beyond[:, :], ALU.max))
                link(v.transpose(picks_t[:, :, :].rearrange("p a g -> p (a g)"), picks[:, :, :].rearrange("p a n -> p (a n)")))
                v.tensor_copy(ib[:, :, :], picks_t[:, 0:2, :])
                link(v.tensor_copy(w_parts[:, 0, :], picks_t[:, 2, :]))
                link(v.tensor_tensor(w_rest[:, :], picks_t[:, 2, :], w_parts[:, 0, :], ALU.subtract))
                link(v.tensor_copy(w_parts[:, 1, :], w_rest[:, :]))
                link(v.tensor_tensor(w_parts[:, 2, :], w_rest[:, :], w_parts[:, 1, :], ALU.subtract))

            def one_hots(j):
                v.tensor_tensor(hot2[:, :, :], iota2[:, :, :], ib[:, 1, :].unsqueeze(1).broadcast_to([128, NK, NG]),
                                ALU.is_equal).then_inc(hot2_ready, 1)
                link(v.tensor_tensor(hot1[:, :, :], iota1[:, :, :, :].rearrange("p j a g -> p (j a) g"),
                                     ib[:, 0, :].unsqueeze(1).broadcast_to([128, 4 * NI1, NG]), ALU.is_equal))
                for part in range(3):
                    v.tensor_tensor(w_hot1[:, part], hot1[:, :, :],
                                    w_parts[:, part, :].unsqueeze(1).broadcast_to([128, 4 * NI1, NG]), ALU.mult).then_inc(hot1_ready, 1)

            def maxima(i, n):
                dve.wait_ge(max_filled, NFILL * i + n + 1)
                bank = score_ps[n % 2]
                if n < 4:
                    dst, src = m_neg[:, 4 * n:4 * n + 4, 0], bank[:, :].rearrange("p (a k) -> p a k", k=K1)
                else:
                    m = n - 4
                    dst = m_neg[:, 2 * m:2 * m + 2, 1]
                    src = bank[:, 0:2 * (K2 + K3)].rearrange("p (a k) -> p a k", k=K2 + K3)
                v.tensor_reduce(dst, src, AX_X, ALU.max, negate=True).then_inc(max_taken, 1)

            def max_parts(i):
                dve.wait_ge(max_transposed, i + 1)
                dve.wait_ge(max_loaded, M_DMAS * i)
                mt = att_ps[0:2 * NP, 2 * T:3 * T]
                link(v.tensor_copy(mt_parts[:, 0, :], mt))
                v.tensor_tensor(mt_parts[:, 1, :], mt, mt_parts[:, 0, :], ALU.subtract).then_inc(max_split, 1)

            def activations(k, c):
                dve.wait_ge(coef_filled, 4 * k + c + 1)
                if c == 0:
                    dve.wait_ge(hs_ready, 4 * k + 4)
                gs = slice(c * 8, c * 8 + 8)
                view = "p a (j g) -> p g j a"
                v.tensor_tensor(act_t[:, :, :].rearrange(view, j=4)[:, gs],
                                coef_ps[c][:, :].rearrange("p (g j a) -> p g j a", j=4, a=NI1),
                                hs[:, :, :].rearrange(view, j=4)[:, gs], ALU.mult).then_inc(act_ready, 1)

            def ffn_tail(k):
                dve.wait_ge(up_done, k + 1)
                v.scalar_tensor_tensor(out=y[:, :], in0=ffn_ps[:, HID:2 * HID], scalar=gates[:, 1:2], in1=x2_last[:, :],
                                       op0=ALU.mult, op1=ALU.add).then_inc(y_ready, 1)

            def att_tail(i):
                dve.wait_ge(pv_done, 4 * i + 4)
                o = o_ps[:, 0:2 * NP * (D + 1)].rearrange("p (n d) -> p n d", d=D + 1)
                link(v.reciprocal(rden[:, :], o[:, :, D]))
                v.tensor_tensor(o_norm[:, :, :], o[:, :, 0:D], rden[:, :].unsqueeze(2).broadcast_to([128, 2 * NP, D]),
                                ALU.mult).then_inc(o_normed, 1)
                dve.wait_ge(wo_done, i + 1)
                dve.wait_ge(res_loaded, 16 * i + 16)
                v.scalar_tensor_tensor(out=x2[:, :], in0=att_ps[:, HID:2 * HID], scalar=gates[:, 0:1], in1=x_res[:, :],
                                       op0=ALU.mult, op1=ALU.add).then_inc(x2_ready, 1)

            def batch(i, att, mid, late):
                j, k = i - 1, i - 2
                if att:
                    dve.wait_ge(x_loaded, 16 * i + 16)
                    norm_stats(x_in, stats, mv, var_eps, var_ready)
                if late:
                    activations(k, 0)
                if att:
                    dve.wait_ge(rstd_ready, i + 1)
                    if mid:
                        dve.wait_ge(xn_transposed, i)
                    norm_apply(x_in, mv, rstd, xn, xn_ready)
                if mid:
                    dve.wait_ge(x2_ready, i)
                    norm_stats(x2, stats2, mv2, var_eps2, var2_ready)
                if late:
                    for c in range(1, 4):
                        activations(k, c)
                if mid:
                    dve.wait_ge(rstd2_ready, j + 1)
                    if late:
                        dve.wait_ge(xn2_transposed, j)
                    norm_apply(x2, mv2, rstd2, xn2, xn2_ready)
                if att:
                    att_parts(i)
                    dve.wait_ge(v_projected, i + 1)
                    if not mid:
                        first_v(0)
                        first_v(1)
                if mid:
                    top(j, att)
                if att:
                    for n in range(NFILL):
                        maxima(i, n)
                    max_parts(i)
                if mid:
                    one_hots(j)
                if late:
                    if not att:
                        dve.wait_ge(out_stored, 16 * k)
                    ffn_tail(k)
                if mid:
                    if late:
                        dve.wait_ge(y_ready, k + 1)
                    link(v.tensor_copy(x2_last[:, :], x2[:, :]))
                if att:
                    att_tail(i)

            dve.wait_ge(gates_ready, 1)
            batch(0, True, False, False)
            restart()
            dve.wait_ge(ffn_w_loaded, 6 * 16)
            batch(1, True, True, False)
            with dve.Fori(2, B) as i:
                restart()
                batch(i, True, True, True)
            restart()
            batch(B, False, True, True)
            batch(B + 1, False, False, True)

        @block.tensor
        def _(pe):
            mm = nc.tensor.matmul

            def att_head(i):
                pe.wait_ge(xn_ready, i + 1)
                pe.wait_ge(o_t_ready, i)
                for k in range(KC):
                    last = nc.tensor.transpose(att_ps[:, k * T:(k + 1) * T], xn[:, k * 128:(k + 1) * 128], ident[:, :])
                last.then_inc(xn_transposed, 1)

            def ffn_head(j):
                pe.wait_ge(xn2_ready, j + 1)
                for k in range(KC):
                    last = nc.tensor.transpose(ffn_ps[:, k * T:(k + 1) * T], xn2[:, k * 128:(k + 1) * 128], ident[:, :])
                last.then_inc(xn2_transposed, 1)

            def project(i):
                pe.wait_ge(ctx_loaded, 16 * i + 16)
                pe.wait_ge(xn_t_ready, i + 1)
                pe.wait_ge(exp_done, NFILL * i)
                src = [ctx_sb, xn_t]
                for c in range(2):
                    for k in range(2 * KC):
                        mm(score_ps[0][:, c * T:(c + 1) * T], wq_sb[:, k, c * 128:(c + 1) * 128],
                           src[k // KC][:, k % KC, :], start=(k == 0), stop=(k == 2 * KC - 1))
                for a in range(2):
                    for k in range(KC):
                        last = mm(score_ps[0][64 * a:64 * a + 64, 2 * T:3 * T], wk_sb[:, a, k, :], src[a][:, k, :],
                                  start=(k == 0), stop=(k == KC - 1))
                last.then_inc(qk_projected, 1)
                n = NKV * D
                for slot, a, rows, lo, m in ((0, 1, 64, 0, 64), (1, 0, 0, 0, T), (2, 1, 0, A3_LO, K3)):
                    for k in range(KC):
                        last = mm(score_ps[1][rows:rows + m, slot * n:(slot + 1) * n], src[a][:, k, lo:lo + m],
                                  wv_sb[:, a, k, :], start=(k == 0), stop=(k == KC - 1))
                last.then_inc(v_projected, 1)

            def sub_keys(j, late):
                pe.wait_ge(xn2_t_ready, j + 1)
                if late:
                    pe.wait_ge(act_ready, 4 * j)
                for h in range(FH):
                    for k in range(KC):
                        last = mm(c_ps[:, h * T:(h + 1) * T], fwq_sb[:, k, h * 128:(h + 1) * 128], xn2_t[:, k, :],
                                  start=(k == 0), stop=(k == KC - 1))
                last.then_inc(fq_projected, 1)
                pe.wait_ge(fq_t_ready, j + 1)
                for h in range(FH):
                    for half in range(2):
                        r = slice(64 * half, 64 * half + 64)
                        last = mm(h_ps[half][:, h * NK:(h + 1) * NK], fq_t[r, h, :], keys_sb[r, h, :], start=True, stop=True)
                last.then_inc(sims_filled, 1)

            def hidden(j, c):
                if c < 2:
                    pe.wait_ge(sims_ready, 2 * j + c + 1)
                else:
                    pe.wait_ge(hs_ready, 4 * j + c - 1)
                for a in range(4):
                    for k in range(KC):
                        at = (4 * c + a) * NK
                        last = mm(h_ps[c % 2][:, a * T:(a + 1) * T], down_sb[:, k, at:at + NK], xn2_t[:, k, :],
                                  start=(k == 0), stop=(k == KC - 1))
                last.then_inc(h_filled, 1)

            def max_scores(i, n):
                if n == 0:
                    pe.wait_ge(operands_loaded, QK_DMAS * (i + 1))
                    pe.wait_ge(rest_ready, i + 1)
                elif n == 1:
                    pe.wait_ge(v_ready, i + 1)
                    pe.wait_ge(first_v_ready, 2 * i + 2)
                else:
                    pe.wait_ge(max_taken, NFILL * i + n - 1)
                qb = 0 if n < 4 else 1
                pairs = range(4 * n, 4 * n + 4) if n < 4 else range(2 * (n - 4), 2 * (n - 4) + 2)
                lo, width = (0, K1) if qb == 0 else (K1, K2 + K3)
                for at, p in enumerate(pairs):
                    last = mm(score_ps[n % 2][:, at * width:(at + 1) * width],
                              q_op[0:R_MAX, p, qb, :],
                              k_op[0:R_MAX, p // 2, lo:lo + width], start=True, stop=True)
                last.then_inc(max_filled, 1)

            def transpose_max(i):
                pe.wait_ge(max_taken, NFILL * i + NFILL)
                pe.wait_ge(x2_ready, i)
                nc.tensor.transpose(att_ps[0:2 * NP, 2 * T:3 * T], m_neg[:, :, :].rearrange("p n b -> p (n b)"),
                                    ident[:, :]).then_inc(max_transposed, 1)

            def coefficients(j, c):
                if c == 0:
                    pe.wait_ge(hot2_ready, j + 1)
                    pe.wait_ge(hot1_ready, 3 * j + 3)
                elif c < 3:
                    pe.wait_ge(hs_ready, 4 * j + 2 + c)
                else:
                    pe.wait_ge(act_ready, 4 * j + 1)
                for gi in range(8):
                    gg = 8 * c + gi
                    for part in range(3):
                        last = mm(coef_ps[c][:, gi * 64:(gi + 1) * 64], hot2[:, :, gg], w_hot1[:, part, :, gg],
                                  start=(part == 0), stop=(part == 2))
                last.then_inc(coef_filled, 1)

            def scores(i, c, s):
                n = 3 * c + s
                if n == 0:
                    pe.wait_ge(max_loaded, M_DMAS * (i + 1))
                if n >= 2:
                    pe.wait_ge(exp_done, NFILL * i + n - 1)
                bank = score_ps[n % 2]
                for at in range(2):
                    kv = 2 * c + (at if s == 2 else s)
                    tile = 2 if s == 2 else at
                    qb = 0 if tile == 0 else 1
                    lo, keys = ((0, K1), (K1, K2), (K1 + K2, K3))[tile]
                    last = mm(bank[0:keys, at * 256:(at + 1) * 256], k_op[:, kv, lo:lo + keys],
                              q_op[:, 2 * kv:2 * kv + 2, qb, :], start=True, stop=True)
                last.then_inc(scores_filled, 1)

            def times_v(i, c):
                pe.wait_ge(exp_done, NFILL * i + 3 * c + 3)
                if c == 0:
                    pe.wait_ge(o_normed, i)
                for h in range(2):
                    kv = 2 * c + h
                    for pair in range(2):
                        p = 2 * kv + pair
                        cols = slice(pair * 128, pair * 128 + 128)
                        cols2 = slice(256 + pair * 128, 256 + pair * 128 + 128)
                        cols3 = slice(h * 256 + pair * 128, h * 256 + pair * 128 + 128)
                        w = D + 1
                        o0, o1 = o_ps[:, p * w:(p + 1) * w], o_ps[:, (NP + p) * w:(NP + p + 1) * w]
                        mm(o0, probs[:, c % 2, h, cols], v_sb[:, 0, kv, :], start=True, stop=True)
                        mm(o1, probs[:, c % 2, h, cols2], v_sb[:, 1, kv, :], start=True, stop=False)
                        last = mm(o1, probs[0:K3, c % 2, 2, cols3], v_sb[0:K3, 2, kv, :], start=False, stop=True)
                last.then_inc(pv_done, 1)

            def up_project(j, a):
                last = mm(ffn_ps[:, HID:2 * HID], act_t[:, a, :], up_sb[:, a, :], start=(a == 0), stop=(a == NI1 - 1))
                if a == NI1 - 1:
                    last.then_inc(up_done, 1)

            def att_tail(i):
                pe.wait_ge(o_normed, i + 1)
                for qb in range(2):
                    last = nc.tensor.transpose(att_ps[:, qb * 128:(qb + 1) * 128],
                                               o_norm[:, qb * NP:(qb + 1) * NP, :].rearrange("p n d -> p (n d)"), ident[:, :])
                last.then_inc(o_transposed, 1)
                pe.wait_ge(o_t_ready, i + 1)
                for h in range(2):
                    last = mm(att_ps[:, HID:2 * HID], o_t[:, h, :], wo_sb[:, h, :], start=(h == 0), stop=(h == 1))
                last.then_inc(wo_done, 1)

            def batch(i, att, mid, late):
                j, k = i - 1, i - 2
                if late:
                    for c in range(4):
                        coefficients(k, c)
                if att:
                    att_head(i)
                    project(i)
                if mid:
                    ffn_head(j)
                    sub_keys(j, late)
                    for c in range(4):
                        hidden(j, c)
                if late:
                    pe.wait_ge(act_ready, 4 * k + 4)
                for n in range(NFILL):
                    if att:
                        max_scores(i, n)
                    if late and n % 3:
                        up_project(k, n // 3 * 2 + n % 3 - 1)
                if att:
                    transpose_max(i)
                if late:
                    for a in range(NI1 // 2, NI1):
                        up_project(k, a)
                if att:
                    for c in range(4):
                        for s in range(3):
                            scores(i, c, s)
                        if c:
                            times_v(i, c - 1)
                    times_v(i, 3)
                    att_tail(i)

            pe.wait_ge(att_w_loaded, 10 * 16)
            pe.wait_ge(wq_scaled, 1)
            pe.wait_ge(setup_done, 2)
            batch(0, True, False, False)
            pe.wait_ge(ffn_w_loaded, 6 * 16)
            batch(1, True, True, False)
            pe.wait_ge(up_loaded, 16)
            with pe.Fori(2, B) as i:
                batch(i, True, True, True)
            batch(B, False, True, True)
            batch(B + 1, False, False, True)


def constants():
    bf = np.dtype("bfloat16")
    keys = np.concatenate([np.arange(QB), np.arange(QB), np.arange(T), np.arange(A3_LO, T)])
    window = np.concatenate([np.full(QB, W_SSM), np.full(QB, W_ATT), np.full(K2, W_SSM), np.full(K3, W_ATT)])
    first = np.concatenate([np.zeros(K1), np.full(K2 + K3, QB)])
    delta = first[None, :] + np.arange(QB)[:, None] - keys[None, :]
    krows = np.concatenate([
        np.broadcast_to(keys, (N_ALIBI, KALL)),
        np.where((delta >= 0) & (delta < window[None, :]), 0.0, MASKED),
        np.ones((N_MAX, KALL)),
    ])
    krows = np.broadcast_to(krows[:, None, :], (ROWS - R_ALIBI, NKV, KALL)).astype(bf)
    slope = np.power(np.float32(2.0), (-8.0 * np.arange(NH, dtype=np.float32) / NH).astype(np.float32)).astype(np.float32)
    rest, parts = slope, []
    for _ in range(N_ALIBI):
        parts.append(rest.astype(bf))
        rest = rest - parts[-1].astype(np.float32)
    qrows = np.zeros((R_MAX - R_ALIBI, NP, 2, 2, QB), bf)
    qrows[:N_ALIBI] = np.stack(parts).reshape(N_ALIBI, NP, 1, 2, 1)
    qrows[N_ALIBI:] = np.eye(QB)[:, None, None, None, :]
    qrows = qrows.reshape(R_MAX - R_ALIBI, NP, 2, 2 * QB)
    iota2 = np.broadcast_to(np.arange(NK)[None, :, None], (128, NK, NG)).astype(bf)
    own = np.arange(128)[:, None] // 32 == np.arange(4)[None, :]
    iota1 = np.where(own[:, :, None], np.arange(NI1)[None, None, :], -1)
    iota1 = np.broadcast_to(iota1[..., None], (128, 4, NI1, NG)).astype(bf)
    return {
        "c_ident": np.eye(128, dtype=np.float32), "c_krows": krows, "c_qrows": qrows,
        "c_iota2": iota2, "c_iota1": iota1,
        "c_ranks": np.broadcast_to(np.arange(FK, dtype=np.float32), (128, FK)),
    }


def kernel(x, ctx_2048, g_xattn, g_ffn, L0_xattn_Wq, L0_xattn_Wk, L0_xattn_Wv, L0_xattn_Wsk, L0_xattn_Wsv,
           L0_xattn_Wo, L0_ffn_Wq, L0_ffn_keys, L0_ffn_e_down, L0_ffn_e_up):
    import concourse.bacc as bacc
    from concourse.bass_utils import run_bass_kernel_spmd

    a = np.asarray
    arrays = {
        "x": a(x),
        "ctx_t": a(ctx_2048).transpose(0, 2, 1).reshape(B, KC, 128, T).transpose(0, 2, 1, 3),
        "g": np.broadcast_to(np.concatenate([a(g_xattn), a(g_ffn)]), (128, 2)),
        "wq": a(L0_xattn_Wq).reshape(2 * HID, NP, 2, D).transpose(0, 2, 3, 1).reshape(2 * HID, HID),
        "wk": a(L0_xattn_Wk).reshape(HID, NKV, D).transpose(0, 2, 1).reshape(HID, NKV * D),
        "wv": a(L0_xattn_Wv),
        "wsk": a(L0_xattn_Wsk).reshape(HID, NKV, D).transpose(0, 2, 1).reshape(HID, NKV * D),
        "wsv": a(L0_xattn_Wsv),
        "wo": a(L0_xattn_Wo).reshape(NP, 2, D, HID).transpose(0, 2, 1, 3).reshape(128, 2, HID),
        "fwq": a(L0_ffn_Wq),
        "keys_t": a(L0_ffn_keys).transpose(2, 3, 0, 1).reshape(2 * DK, FH, NK),
        "down_t": a(L0_ffn_e_down).T, "up": a(L0_ffn_e_up),
        **constants(),
    }
    nc = bacc.Bacc("TRN2", target_bir_lowering=False, num_devices=1)
    aps = []
    for name, v in arrays.items():
        arrays[name] = v = np.ascontiguousarray(v)
        aps.append(nc.dram_tensor(name, v.shape, mybir.dt.from_np(v.dtype), kind="ExternalInput").ap())
    aps.append(nc.dram_tensor("out", (B, T, HID), F32, kind="ExternalOutput").ap())
    program(nc, *aps)
    r = run_bass_kernel_spmd(nc, [arrays], core_ids=[0])
    return r.results[0]["out"]
```

```python
from contextlib import ExitStack

import numpy as np

import concourse.bass as bass
from concourse import mybir

F32 = mybir.dt.float32
BF16 = mybir.dt.bfloat16
U32 = mybir.dt.uint32
ALU = mybir.AluOpType
ACT = mybir.ActivationFunctionType
AX_X = mybir.AxisListType.X

B, T, HID = 16, 128, 256
KC = HID // 128
NH, NKV, D = 32, 8, 8
NP = NH // 2
W_SSM, W_ATT = 64, 32
QB = 64
K1, K2, K3 = 128, 128, 96
KALL = K1 + K2 + K3
A3_LO = T - K3
Q_PART = [0, 0, 0, 1, 1, 2]
K_RUNS = [(0, 3), (3, 2), (5, 1)]
R_QK = len(Q_PART) * D
R_ALIBI, N_ALIBI = R_QK, 3
R_MASK = R_ALIBI + N_ALIBI
R_MAX, N_MAX = R_MASK + QB, 2
ROWS = R_MAX + N_MAX
MASKED = -1e30
FH, FK, DK, NK, E = 4, 8, 64, 128, 2048
NI1 = E // NK
NPICK = FH * FK
NG = T // 4
EPS = 1e-5

STORES = 5 * 16
QK_DMAS = (len(Q_PART) + len(K_RUNS)) * 16
M_DMAS = N_MAX * 16
N_STREAM = 7
O_COLS = [0, (NP + N_STREAM - 1) * (D + 1)]
UP_QUERY, UP_SIMS, UP_MAX, UP_SPLIT = 2, 3, 7, 12
NFILL = 12


def past(i, n):
    return not isinstance(i, int) or i >= n


def program(nc, x, ctx_t, g, wq, wk, wv, wsk, wsv, wo, fwq, keys_t, down_t, up,
            c_ident, c_krows, c_qrows, c_iota2, c_iota1, c_ranks, out):
    st = ExitStack()
    with st:
        def sb(name, shape, dt=F32):
            return st.enter_context(nc.sbuf_tensor(name, shape, dt))

        def ps(name):
            return st.enter_context(nc.psum_tensor(name, [128, 512], F32))

        def sem(name):
            return st.enter_context(nc.semaphore(name))

        wq_sb = sb("wq_sb", [128, 2 * KC, HID])
        wk_sb = sb("wk_sb", [128, 2, KC, NKV * D])
        wv_sb = sb("wv_sb", [128, 2, KC, NKV * D])
        wo_sb = sb("wo_sb", [128, 2, HID])
        fwq_sb = sb("fwq_sb", [128, KC, 2 * FH * DK])
        keys_sb = sb("keys_sb", [128, FH, NK])
        down_sb = sb("down_sb", [128, KC, E])
        up_sb = sb("up_sb", [128, NI1, HID])
        ident = sb("ident", [128, 128])
        iota2 = sb("iota2", [128, NK, NG], BF16)
        iota1 = sb("iota1", [128, 4, NI1, NG], BF16)
        ranks = sb("ranks", [128, FK])
        gates = sb("gates", [128, 2])
        half_neg = sb("half_neg", [128, 1])

        x_in = sb("x_in", [128, HID])
        x_res = sb("x_res", [128, HID])
        ctx_sb = sb("ctx_sb", [128, KC, T])
        stats = sb("stats", [128, 6])
        mv = sb("mv", [128, 2])
        var_eps = sb("var_eps", [128, 1])
        rstd = sb("rstd", [128, 1])
        xn = sb("xn", [128, HID])
        xn_t = sb("xn_t", [128, KC, T])
        qk_parts = sb("qk_parts", [128, 3, 3 * T], BF16)
        qk_rest = sb("qk_rest", [128, 3 * T])
        q_op = sb("q_op", [ROWS, NP, 2, 2 * QB], BF16)
        k_op = sb("k_op", [ROWS, NKV, KALL], BF16)
        v_sb = sb("v_sb", [128, 3, NKV + N_STREAM - 1, D + 1])
        m_neg = sb("m_neg", [128, NP, 2])
        mt_parts = sb("mt_parts", [2 * NP, N_MAX, 128], BF16)
        probs = sb("probs", [128, 2, 3, 512])
        rden = sb("rden", [128, 2, NP])
        o_norm = sb("o_norm", [128, 2, NP, D])
        o_t = sb("o_t", [128, 2, T])
        x2 = sb("x2", [128, HID])
        x2_last = sb("x2_last", [128, HID])

        stats2 = sb("stats2", [128, 6])
        mv2 = sb("mv2", [128, 2])
        var_eps2 = sb("var_eps2", [128, 1])
        rstd2 = sb("rstd2", [128, 1])
        xn2 = sb("xn2", [128, HID])
        xn2_t = sb("xn2_t", [128, KC, T])
        fq_t = sb("fq_t", [128, FH, T])
        sims = sb("sims", [128, 2, FH, NK])
        top_s = sb("top_s", [128, 2, FH, FK])
        top_i = sb("top_i", [128, 2, FH, FK], U32)
        top_if = sb("top_if", [128, 2 * FH, FK])
        pair_s = sb("pair_s", [128, FH, FK, FK])
        fin_s = sb("fin_s", [128, FH, FK])
        fin_i = sb("fin_i", [128, NPICK], U32)
        rank12 = sb("rank12", [128, 2, NPICK], U32)
        hot_r = sb("hot_r", [128, 2 * NPICK, FK])
        val_r = sb("val_r", [128, 2 * NPICK, FK])
        pick_i = sb("pick_i", [128, 2, NPICK])
        beyond = sb("beyond", [128, NPICK])
        picks = sb("picks", [128, 3, NPICK])
        picks_t = sb("picks_t", [128, 3, NG])
        ib = sb("ib", [128, 2, NG], BF16)
        w_parts = sb("w_parts", [128, 3, NG], BF16)
        w_rest = sb("w_rest", [128, NG])
        hot2 = sb("hot2", [128, NK, NG], BF16)
        hot1 = sb("hot1", [128, 4 * NI1, NG], BF16)
        w_hot1 = sb("w_hot1", [128, 3, 4 * NI1, NG], BF16)
        hs = sb("hs", [128, NI1, T])
        act_t = sb("act_t", [128, NI1, T])
        y = sb("y", [128, HID])

        q_scratch = nc.dram_tensor("q_scratch", (3, D, NP, 2 * T), BF16, kind="Internal").ap()
        k_scratch = nc.dram_tensor("k_scratch", (3, D, NKV, KALL), BF16, kind="Internal").ap()

        score_ps = [ps("score_ps0"), ps("score_ps1")]
        o_ps = ps("o_ps")
        att_ps = ps("att_ps")
        h_ps = [ps("h_ps0"), ps("h_ps1")]
        c_ps = ps("c_ps")
        ffn_ps = ps("ffn_ps")
        coef_ps = [h_ps[0], h_ps[1], c_ps, h_ps[0]]

        att_w_loaded = sem("att_w_loaded")
        ffn_w_loaded = sem("ffn_w_loaded")
        up_loaded = sem("up_loaded")
        x_loaded = sem("x_loaded")
        ctx_loaded = sem("ctx_loaded")
        res_loaded = sem("res_loaded")
        parts_stored = sem("parts_stored")
        operands_loaded = sem("operands_loaded")
        max_loaded = sem("max_loaded")
        out_stored = sem("out_stored")
        setup_done = sem("setup_done")
        wq_scaled = sem("wq_scaled")
        gates_ready = sem("gates_ready")
        var_ready = sem("var_ready")
        rstd_ready = sem("rstd_ready")
        xn_ready = sem("xn_ready")
        xn_transposed = sem("xn_transposed")
        xn_t_ready = sem("xn_t_ready")
        qk_projected = sem("qk_projected")
        v_projected = sem("v_projected")
        v_ready = sem("v_ready")
        first_v_ready = sem("first_v_ready")
        hi_ready = sem("hi_ready")
        rest_ready = sem("rest_ready")
        mid_ready = sem("mid_ready")
        parts_ready = sem("parts_ready")
        max_filled = sem("max_filled")
        max_taken = sem("max_taken")
        max_transposed = sem("max_transposed")
        max_split = sem("max_split")
        scores_filled = sem("scores_filled")
        exp_done = sem("exp_done")
        pv_done = sem("pv_done")
        o_normed = sem("o_normed")
        o_transposed = sem("o_transposed")
        o_t_ready = sem("o_t_ready")
        wo_done = sem("wo_done")
        x2_ready = sem("x2_ready")
        var2_ready = sem("var2_ready")
        rstd2_ready = sem("rstd2_ready")
        xn2_ready = sem("xn2_ready")
        xn2_transposed = sem("xn2_transposed")
        xn2_t_ready = sem("xn2_t_ready")
        fq_projected = sem("fq_projected")
        fq_t_ready = sem("fq_t_ready")
        sims_filled = sem("sims_filled")
        sims_ready = sem("sims_ready")
        hot2_ready = sem("hot2_ready")
        hot1_ready = sem("hot1_ready")
        h_filled = sem("h_filled")
        hs_ready = sem("hs_ready")
        coef_filled = sem("coef_filled")
        act_ready = sem("act_ready")
        up_done = sem("up_done")
        y_ready = sem("y_ready")
        dve_step = sem("dve_step")

        block = st.enter_context(nc.Block())

        @block.sync
        def _(sp):
            def load(dst, src, s):
                sp.dma_start(dst, src).then_inc(s, 16)

            load(x_in[:, :], x[0, :, :], x_loaded)
            load(ctx_sb[:, :, :], ctx_t[0, :, :, :], ctx_loaded)
            load(ident[:, :], c_ident[:, :], att_w_loaded)
            load(wq_sb[:, :, :], wq.rearrange("(k p) n -> p k n", p=128), att_w_loaded)
            for a, (kk, vv) in enumerate(((wsk, wsv), (wk, wv))):
                load(wk_sb[:, a], kk.rearrange("(k p) n -> p k n", p=128), att_w_loaded)
                load(wv_sb[:, a], vv.rearrange("(k p) n -> p k n", p=128), att_w_loaded)
            load(k_op[R_ALIBI:ROWS, :, :], c_krows[:, :, :], att_w_loaded)
            load(q_op[R_ALIBI:R_MAX, :, :, :], c_qrows[:, :, :, :], att_w_loaded)
            load(wo_sb[:, :, :], wo[:, :, :], att_w_loaded)
            load(gates[:, :], g[:, :], att_w_loaded)

            def operands(i):
                sp.wait_ge(parts_ready, i + 1)
                load(q_scratch.rearrange("a d n t -> (d n) a t"), qk_parts[:, :, 0:2 * T], parts_stored)
                for a, lo, n, at in ((0, 0, QB, 0), (1, 0, QB, QB), (0, 0, T, K1), (1, A3_LO, K3, K1 + K2)):
                    load(k_scratch[:, :, :, at:at + n].rearrange("a d n t -> (d n) a t"),
                         qk_parts[64 * a:64 * a + 64, :, 2 * T + lo:2 * T + lo + n], parts_stored)
                sp.wait_ge(parts_stored, STORES * (i + 1))
                for r, pq in enumerate(Q_PART):
                    load(q_op[D * r:D * r + D, :, :, :].rearrange("r p b t -> r (p b t)"),
                         q_scratch[pq].rearrange("d n t -> d (n t)"), operands_loaded)
                for r, n in K_RUNS:
                    load(k_op[D * r:D * (r + n), :, :].rearrange("r n t -> r (n t)"),
                         k_scratch[0:n].rearrange("a d n t -> (a d) (n t)"), operands_loaded)

            def prefetch(i):
                sp.wait_ge(xn_ready, i)
                load(x_in[:, :], x[i, :, :], x_loaded)
                sp.wait_ge(v_projected, i)
                load(ctx_sb[:, :, :], ctx_t[i, :, :, :], ctx_loaded)

            def residual(i):
                sp.wait_ge(x2_ready, i)
                load(x_res[:, :], x[i, :, :], res_loaded)

            def maxima(i):
                sp.wait_ge(max_split, i + 1)
                for part in range(N_MAX):
                    row = R_MAX + part
                    load(q_op[row:row + 1, :, :, :].rearrange("r p b t -> r (p b) t"), mt_parts[:, part, :], max_loaded)

            def store(j):
                sp.wait_ge(y_ready, j + 1)
                sp.dma_start(out[j, :, :], y[:, :]).then_inc(out_stored, 16)

            operands(0)
            load(fwq_sb[:, :, :], fwq.rearrange("(k p) n -> p k n", p=128), ffn_w_loaded)
            load(keys_sb[:, :, :], keys_t[:, :, :], ffn_w_loaded)
            load(ranks[:, :], c_ranks[:, :], ffn_w_loaded)
            prefetch(1)
            load(x_res[:, :], x[0, :, :], res_loaded)
            load(down_sb[:, :, :], down_t.rearrange("(k p) n -> p k n", p=128), ffn_w_loaded)
            load(iota2[:, :, :], c_iota2[:, :, :], ffn_w_loaded)
            load(iota1[:, :, :, :], c_iota1[:, :, :, :], ffn_w_loaded)
            maxima(0)
            load(up_sb[:, :, :], up.rearrange("(a p) n -> p a n", p=128), up_loaded)
            for i in (1, 2):
                operands(i)
                prefetch(i + 1)
                residual(i)
                maxima(i)
            with sp.Fori(3, B - 1) as i:
                store(i - 3)
                operands(i)
                sp.wait_ge(out_stored, 16 * (i - 2))
                prefetch(i + 1)
                residual(i)
                maxima(i)
            store(B - 4)
            operands(B - 1)
            residual(B - 1)
            maxima(B - 1)
            for j in range(B - 3, B):
                store(j)
            sp.wait_ge(out_stored, 16 * B)

        @block.gpsimd
        def _(pool):
            pool.memset(half_neg[:, :], -0.5).then_inc(setup_done, 1)
            pool.memset(v_sb[:, :, :, :], 1.0).then_inc(setup_done, 1)
            pool.wait_ge(setup_done, 1)

            def norm1(i):
                pool.wait_ge(var_ready, i + 1)
                pool.tensor_tensor(rstd[:, :], var_eps[:, :], half_neg[:, :], ALU.pow).then_inc(rstd_ready, 1)

            def norm2(i):
                pool.wait_ge(var2_ready, i + 1)
                pool.tensor_tensor(rstd2[:, :], var_eps2[:, :], half_neg[:, :], ALU.pow).then_inc(rstd2_ready, 1)

            norm1(0)
            with pool.Fori(1, B) as i:
                norm1(i)
                norm2(i - 1)
            norm2(B - 1)

        @block.scalar
        def _(act):
            act.wait_ge(att_w_loaded, 10 * 16)
            nc.scalar.mul(wq_sb[:, :, :], wq_sb[:, :, :], float(D) ** -0.5).then_inc(wq_scaled, 1)
            nc.scalar.activation(gates[:, :], gates[:, :], ACT.Tanh).then_inc(gates_ready, 1)
            act.wait_ge(setup_done, 2)

            def att_head(i):
                act.wait_ge(xn_transposed, i + 1)
                nc.scalar.copy(xn_t[:, :, :], att_ps[:, 0:KC * T].rearrange("p (k t) -> p k t", t=T)).then_inc(xn_t_ready, 1)

            def att_parts(i, mid):
                act.wait_ge(qk_projected, i + 1)
                act.wait_ge(parts_stored, STORES * i)
                blocks = "p (h b q) -> p b h q"
                nc.scalar.copy(qk_parts[:, 0, 0:2 * T].rearrange("p (b h q) -> p b h q", b=2, h=2),
                               score_ps[0][:, 0:2 * T].rearrange(blocks, h=2, b=2))
                nc.scalar.copy(qk_parts[:, 0, 2 * T:3 * T], score_ps[0][:, 2 * T:3 * T]).then_inc(hi_ready, 1)
                if mid:
                    att_tail(i - 1)
                act.wait_ge(rest_ready, i + 1)
                nc.scalar.copy(qk_parts[:, 1, :], qk_rest[:, :]).then_inc(mid_ready, 1)
                act.wait_ge(v_projected, i + 1)
                v = score_ps[1][:, 0:3 * NKV * D].rearrange("p (n h d) -> p n h d", n=3, d=D)
                nc.scalar.copy(v_sb[:, 1, 0:NKV, 0:D], v[:, 1])
                nc.scalar.copy(v_sb[0:K3, 2, 0:NKV, 0:D], v[0:K3, 2]).then_inc(v_ready, 1)

            def ffn_head(j):
                act.wait_ge(xn2_transposed, j + 1)
                nc.scalar.copy(xn2_t[:, :, :], ffn_ps[:, 0:KC * T].rearrange("p (k t) -> p k t", t=T)).then_inc(xn2_t_ready, 1)

            def ffn_sims(j):
                act.wait_ge(fq_projected, j + 1)
                nc.scalar.copy(fq_t[:, :, :], c_ps[:, :].rearrange("p (h t) -> p h t", t=T)).then_inc(fq_t_ready, 1)
                act.wait_ge(sims_filled, j + 1)
                for half in range(2):
                    nc.scalar.copy(sims[:, half], h_ps[half][:, :].rearrange("p (h n) -> p h n", n=NK)).then_inc(sims_ready, 1)

            def silus(j):
                for c in range(4):
                    act.wait_ge(h_filled, 4 * j + c + 1)
                    nc.scalar.activation(hs[:, 4 * c:4 * c + 4, :].rearrange("p a t -> p (a t)"), h_ps[c % 2][:, :],
                                         ACT.Silu).then_inc(hs_ready, 1)

            def exps(i):
                for c in range(4):
                    if c or past(i, 1):
                        act.wait_ge(pv_done, 4 * i + c - 1)
                    for s in range(3):
                        n = 3 * c + s
                        keys = K3 if s == 2 else 128
                        act.wait_ge(scores_filled, NFILL * i + n + 1)
                        nc.scalar.activation(probs[0:keys, c % 2, s, :], score_ps[n % 2][0:keys, :], ACT.Exp).then_inc(exp_done, 1)

            def att_tail(i):
                act.wait_ge(o_transposed, i + 1)
                src = att_ps[:, 0:2 * 128].rearrange("p (b h q) -> p h b q", b=2, h=2)
                nc.scalar.copy(o_t[:, :, :].rearrange("p h (b q) -> p h b q", b=2), src).then_inc(o_t_ready, 1)

            def batch(i, att, mid):
                if mid:
                    exps(i - 1)
                if att:
                    att_head(i)
                    att_parts(i, mid)
                if mid:
                    if not att:
                        att_tail(i - 1)
                    ffn_head(i - 1)
                    ffn_sims(i - 1)
                    silus(i - 1)

            batch(0, True, False)
            batch(1, True, True)
            with act.Fori(2, B) as i:
                batch(i, True, True)
            batch(B, False, True)

        @block.vector
        def _(dve):
            v = nc.vector
            steps = {"n": 0}

            def link(ins):
                steps["n"] += 1
                ins.then_inc(dve_step, 1)
                dve.wait_ge(dve_step, steps["n"])

            def restart():
                dve.sem_clear(dve_step)
                steps["n"] = 0

            def norm_stats(src, stats, mv, var_eps, var_sem):
                link(v.bn_stats(stats[:, :], src[:, :]))
                link(v.bn_aggr(mv[:, :], stats[:, :]))
                v.tensor_scalar_add(var_eps[:, :], mv[:, 1:2], EPS).then_inc(var_sem, 1)

            def norm_apply(src, mv, rstd, xn, sem):
                v.tensor_scalar(xn[:, :], src[:, :], mv[:, 0:1], rstd[:, 0:1], ALU.subtract, ALU.mult).then_inc(sem, 1)

            def att_parts(i):
                dve.wait_ge(hi_ready, i + 1)
                blocks, put = "p (h b q) -> p b h q", "p (b h q) -> p b h q"
                v.tensor_tensor(qk_rest[:, 0:2 * T].rearrange(put, b=2, h=2), score_ps[0][:, 0:2 * T].rearrange(blocks, h=2, b=2),
                                qk_parts[:, 0, 0:2 * T].rearrange(put, b=2, h=2), ALU.subtract)
                v.tensor_tensor(qk_rest[:, 2 * T:3 * T], score_ps[0][:, 2 * T:3 * T], qk_parts[:, 0, 2 * T:3 * T],
                                ALU.subtract).then_inc(rest_ready, 1)
                dve.wait_ge(mid_ready, i + 1)
                v.tensor_tensor(qk_parts[:, 2, :], qk_rest[:, :], qk_parts[:, 1, :], ALU.subtract).then_inc(parts_ready, 1)

            def first_v(upper):
                r = slice(64 * upper, 64 * upper + 64)
                src = score_ps[1][r, (1 - upper) * NKV * D:(2 - upper) * NKV * D]
                v.tensor_copy(v_sb[r, 0, 0:NKV, 0:D], src.rearrange("p (h d) -> p h d", d=D)).then_inc(first_v_ready, 1)

            def top(j):
                for half in range(2):
                    for h in range(FH):
                        last = v.max(top_s[:, half, h], sims[:, half, h])
                link(last)
                for half in range(2):
                    for h in range(FH):
                        last = v.max_index(top_i[:, half, h], top_s[:, half, h], sims[:, half, h])
                link(v.tensor_tensor(pair_s[:, :, :, :], top_s[:, 0].unsqueeze(3).broadcast_to([128, FH, FK, FK]),
                                     top_s[:, 1].unsqueeze(2).broadcast_to([128, FH, FK, FK]), ALU.add))
                v.tensor_copy(top_if[:, :, :], top_i[:, :, :, :].rearrange("p a h k -> p (a h) k"))
                for h in range(FH):
                    last = v.max(fin_s[:, h], pair_s[:, h].rearrange("p a b -> p (a b)"))
                link(last)
                for h in range(FH):
                    last = v.max_index(fin_i[:, h * FK:(h + 1) * FK], fin_s[:, h], pair_s[:, h].rearrange("p a b -> p (a b)"))
                link(last)
                v.tensor_scalar(rank12[:, 0, :], fin_i[:, :], 3, None, ALU.logical_shift_right)
                link(v.tensor_scalar(rank12[:, 1, :], fin_i[:, :], FK - 1, None, ALU.bitwise_and))
                link(v.tensor_tensor(hot_r[:, :, :],
                                     rank12[:, :, :].rearrange("p a n -> p (a n)").unsqueeze(2).broadcast_to([128, 2 * NPICK, FK]),
                                     ranks[:, :].unsqueeze(1).broadcast_to([128, 2 * NPICK, FK]), ALU.is_equal))
                link(v.tensor_tensor(val_r[:, :, :].rearrange("p (a k) r -> p a k r", k=FK),
                                     hot_r[:, :, :].rearrange("p (a k) r -> p a k r", k=FK),
                                     top_if[:, :, :].unsqueeze(2).broadcast_to([128, 2 * FH, FK, FK]), ALU.mult))
                link(v.tensor_reduce(pick_i[:, :, :].rearrange("p a n -> p (a n)"), val_r[:, :, :], AX_X, ALU.add))
                v.tensor_scalar(beyond[:, :], pick_i[:, 0, :], float(NI1), float(NK - 1), ALU.is_ge, ALU.mult)
                v.tensor_scalar(picks[:, 0, :], pick_i[:, 0, :], float(NI1 - 1), None, ALU.min)
                link(v.tensor_scalar(picks[:, 2, :], fin_s[:, :, :].rearrange("p h k -> p (h k)"), 0.0, None, ALU.max))
                link(v.tensor_tensor(picks[:, 1, :], pick_i[:, 1, :], beyond[:, :], ALU.max))
                link(v.transpose(picks_t[:, :, :].rearrange("p a g -> p (a g)"), picks[:, :, :].rearrange("p a n -> p (a n)")))
                v.tensor_copy(ib[:, :, :], picks_t[:, 0:2, :])
                link(v.tensor_copy(w_parts[:, 0, :], picks_t[:, 2, :]))
                link(v.tensor_tensor(w_rest[:, :], picks_t[:, 2, :], w_parts[:, 0, :], ALU.subtract))
                link(v.tensor_copy(w_parts[:, 1, :], w_rest[:, :]))
                link(v.tensor_tensor(w_parts[:, 2, :], w_rest[:, :], w_parts[:, 1, :], ALU.subtract))

            def one_hots(j):
                v.tensor_tensor(hot2[:, :, :], iota2[:, :, :], ib[:, 1, :].unsqueeze(1).broadcast_to([128, NK, NG]),
                                ALU.is_equal).then_inc(hot2_ready, 1)
                link(v.tensor_tensor(hot1[:, :, :], iota1[:, :, :, :].rearrange("p j a g -> p (j a) g"),
                                     ib[:, 0, :].unsqueeze(1).broadcast_to([128, 4 * NI1, NG]), ALU.is_equal))
                for part in range(3):
                    v.tensor_tensor(w_hot1[:, part], hot1[:, :, :],
                                    w_parts[:, part, :].unsqueeze(1).broadcast_to([128, 4 * NI1, NG]), ALU.mult).then_inc(hot1_ready, 1)

            def maxima(i, n):
                dve.wait_ge(max_filled, NFILL * i + n + 1)
                bank = score_ps[n % 2]
                if n < 4:
                    dst, src = m_neg[:, 4 * n:4 * n + 4, 0], bank[:, :].rearrange("p (a k) -> p a k", k=K1)
                else:
                    m = n - 4
                    dst = m_neg[:, 2 * m:2 * m + 2, 1]
                    src = bank[:, 0:2 * (K2 + K3)].rearrange("p (a k) -> p a k", k=K2 + K3)
                v.tensor_reduce(dst, src, AX_X, ALU.max, negate=True).then_inc(max_taken, 1)

            def max_parts(i):
                dve.wait_ge(max_transposed, i + 1)
                dve.wait_ge(max_loaded, M_DMAS * i)
                mt = att_ps[0:2 * NP, 2 * T:3 * T]
                link(v.tensor_copy(mt_parts[:, 0, :], mt))
                v.tensor_tensor(mt_parts[:, 1, :], mt, mt_parts[:, 0, :], ALU.subtract).then_inc(max_split, 1)

            def activations(k, c):
                dve.wait_ge(coef_filled, 4 * k + c + 1)
                if c == 0:
                    dve.wait_ge(hs_ready, 4 * k + 4)
                gs = slice(c * 8, c * 8 + 8)
                view = "p a (j g) -> p g j a"
                v.tensor_tensor(act_t[:, :, :].rearrange(view, j=4)[:, gs],
                                coef_ps[c][:, :].rearrange("p (g j a) -> p g j a", j=4, a=NI1),
                                hs[:, :, :].rearrange(view, j=4)[:, gs], ALU.mult).then_inc(act_ready, 1)

            def ffn_tail(k):
                dve.wait_ge(up_done, k + 1)
                v.scalar_tensor_tensor(out=y[:, :], in0=ffn_ps[:, HID:2 * HID], scalar=gates[:, 1:2], in1=x2_last[:, :],
                                       op0=ALU.mult, op1=ALU.add).then_inc(y_ready, 1)

            def att_normalise(i):
                dve.wait_ge(pv_done, 4 * i + 4)
                o = [o_ps[:, at:at + NP * (D + 1)].rearrange("p (n d) -> p n d", d=D + 1) for at in O_COLS]
                v.reciprocal(rden[:, 0], o[0][:, :, D])
                link(v.reciprocal(rden[:, 1], o[1][:, :, D]))
                for qb in range(2):
                    v.tensor_tensor(o_norm[:, qb], o[qb][:, :, 0:D], rden[:, qb].unsqueeze(2).broadcast_to([128, NP, D]),
                                    ALU.mult).then_inc(o_normed, 1)

            def att_residual(i):
                dve.wait_ge(wo_done, i + 1)
                dve.wait_ge(res_loaded, 16 * i + 16)
                v.scalar_tensor_tensor(out=x2[:, :], in0=att_ps[:, HID:2 * HID], scalar=gates[:, 0:1], in1=x_res[:, :],
                                       op0=ALU.mult, op1=ALU.add).then_inc(x2_ready, 1)

            def batch(i, att, mid, late, last):
                j, k = i - 1, i - 2
                if att:
                    dve.wait_ge(x_loaded, 16 * i + 16)
                    norm_stats(x_in, stats, mv, var_eps, var_ready)
                    dve.wait_ge(rstd_ready, i + 1)
                    if mid:
                        dve.wait_ge(xn_transposed, i)
                    if late:
                        dve.wait_ge(sims_ready, 2 * k + 2)
                    norm_apply(x_in, mv, rstd, xn, xn_ready)
                if late:
                    if not att:
                        dve.wait_ge(sims_ready, 2 * k + 2)
                    top(k)
                    one_hots(k)
                if last:
                    if not att:
                        dve.wait_ge(out_stored, 16 * (i - 3))
                    ffn_tail(i - 3)
                    dve.wait_ge(y_ready, i - 2)
                if late:
                    link(v.tensor_copy(x2_last[:, :], x2[:, :]))
                if mid:
                    att_normalise(j)
                if att:
                    att_parts(i)
                if mid:
                    att_residual(j)
                    dve.wait_ge(x2_ready, j + 1)
                    norm_stats(x2, stats2, mv2, var_eps2, var2_ready)
                if late:
                    activations(k, 0)
                if mid:
                    dve.wait_ge(rstd2_ready, j + 1)
                    if late:
                        dve.wait_ge(xn2_transposed, j)
                    norm_apply(x2, mv2, rstd2, xn2, xn2_ready)
                if late:
                    for c in range(1, 4):
                        activations(k, c)
                if att:
                    dve.wait_ge(v_ready, i + 1)
                    first_v(0)
                    first_v(1)
                    for n in range(NFILL):
                        maxima(i, n)
                    max_parts(i)

            dve.wait_ge(gates_ready, 1)
            batch(0, True, False, False, False)
            restart()
            dve.wait_ge(ffn_w_loaded, 6 * 16)
            batch(1, True, True, False, False)
            restart()
            batch(2, True, True, True, False)
            with dve.Fori(3, B) as i:
                restart()
                batch(i, True, True, True, True)
            restart()
            batch(B, False, True, True, True)
            batch(B + 1, False, False, True, True)
            batch(B + 2, False, False, False, True)

        @block.tensor
        def _(pe):
            mm = nc.tensor.matmul

            def transpose_xn(i):
                pe.wait_ge(xn_ready, i + 1)
                if past(i, 2):
                    pe.wait_ge(o_t_ready, i - 1)
                for k in range(KC):
                    last = nc.tensor.transpose(att_ps[:, k * T:(k + 1) * T], xn[:, k * 128:(k + 1) * 128], ident[:, :])
                last.then_inc(xn_transposed, 1)

            def ffn_head(j):
                pe.wait_ge(xn2_ready, j + 1)
                for k in range(KC):
                    last = nc.tensor.transpose(ffn_ps[:, k * T:(k + 1) * T], xn2[:, k * 128:(k + 1) * 128], ident[:, :])
                last.then_inc(xn2_transposed, 1)

            def project(i):
                pe.wait_ge(ctx_loaded, 16 * i + 16)
                pe.wait_ge(xn_t_ready, i + 1)
                if past(i, 1):
                    pe.wait_ge(exp_done, NFILL * i)
                src = [ctx_sb, xn_t]
                for c in range(2):
                    for k in range(2 * KC):
                        mm(score_ps[0][:, c * T:(c + 1) * T], wq_sb[:, k, c * 128:(c + 1) * 128],
                           src[k // KC][:, k % KC, :], start=(k == 0), stop=(k == 2 * KC - 1))
                for a in range(2):
                    for k in range(KC):
                        last = mm(score_ps[0][64 * a:64 * a + 64, 2 * T:3 * T], wk_sb[:, a, k, :], src[a][:, k, :],
                                  start=(k == 0), stop=(k == KC - 1))
                last.then_inc(qk_projected, 1)
                n = NKV * D
                for slot, a, rows, lo, m in ((0, 1, 64, 0, 64), (1, 0, 0, 0, T), (2, 1, 0, A3_LO, K3)):
                    for k in range(KC):
                        last = mm(score_ps[1][rows:rows + m, slot * n:(slot + 1) * n], src[a][:, k, lo:lo + m],
                                  wv_sb[:, a, k, :], start=(k == 0), stop=(k == KC - 1))
                last.then_inc(v_projected, 1)

            def query(j, late):
                pe.wait_ge(xn2_t_ready, j + 1)
                if late:
                    pe.wait_ge(act_ready, 4 * j - 1)
                for h in range(FH):
                    for k in range(KC):
                        last = mm(c_ps[:, h * T:(h + 1) * T], fwq_sb[:, k, h * 128:(h + 1) * 128], xn2_t[:, k, :],
                                  start=(k == 0), stop=(k == KC - 1))
                last.then_inc(fq_projected, 1)

            def sub_keys(j, late):
                pe.wait_ge(fq_t_ready, j + 1)
                if late:
                    pe.wait_ge(act_ready, 4 * j)
                for h in range(FH):
                    for half in range(2):
                        r = slice(64 * half, 64 * half + 64)
                        last = mm(h_ps[half][:, h * NK:(h + 1) * NK], fq_t[r, h, :], keys_sb[r, h, :], start=True, stop=True)
                last.then_inc(sims_filled, 1)

            def hidden(j, a):
                c = a // 4
                if a == 4 * c:
                    if c < 2:
                        pe.wait_ge(sims_ready, 2 * j + c + 1)
                    else:
                        pe.wait_ge(hs_ready, 4 * j + c - 1)
                for k in range(KC):
                    last = mm(h_ps[c % 2][:, a % 4 * T:(a % 4 + 1) * T], down_sb[:, k, a * NK:(a + 1) * NK],
                              xn2_t[:, k, :], start=(k == 0), stop=(k == KC - 1))
                if a == 4 * c + 3:
                    last.then_inc(h_filled, 1)

            def max_scores(i, n):
                if n == 0:
                    pe.wait_ge(operands_loaded, QK_DMAS * (i + 1))
                    pe.wait_ge(rest_ready, i + 1)
                elif n == 1:
                    pe.wait_ge(first_v_ready, 2 * i + 2)
                else:
                    pe.wait_ge(max_taken, NFILL * i + n - 1)
                qb = 0 if n < 4 else 1
                pairs = range(4 * n, 4 * n + 4) if n < 4 else range(2 * (n - 4), 2 * (n - 4) + 2)
                lo, width = (0, K1) if qb == 0 else (K1, K2 + K3)
                for at, p in enumerate(pairs):
                    last = mm(score_ps[n % 2][:, at * width:(at + 1) * width],
                              q_op[0:R_MAX, p, qb, :],
                              k_op[0:R_MAX, p // 2, lo:lo + width], start=True, stop=True)
                last.then_inc(max_filled, 1)

            def transpose_max(i):
                pe.wait_ge(max_taken, NFILL * i + NFILL)
                if past(i, 1):
                    pe.wait_ge(x2_ready, i)
                nc.tensor.transpose(att_ps[0:2 * NP, 2 * T:3 * T], m_neg[:, :, :].rearrange("p n b -> p (n b)"),
                                    ident[:, :]).then_inc(max_transposed, 1)

            def coefficients(j, c):
                if c == 0:
                    pe.wait_ge(hot2_ready, j + 1)
                    pe.wait_ge(hot1_ready, 3 * j + 3)
                    pe.wait_ge(hs_ready, 4 * j + 4)
                elif c == 3:
                    pe.wait_ge(act_ready, 4 * j + 1)
                for gi in range(8):
                    gg = 8 * c + gi
                    for part in range(3):
                        last = mm(coef_ps[c][:, gi * 64:(gi + 1) * 64], hot2[:, :, gg], w_hot1[:, part, :, gg],
                                  start=(part == 0), stop=(part == 2))
                last.then_inc(coef_filled, 1)

            def scores(i, n):
                c, s = n // 3, n % 3
                if n == 0:
                    pe.wait_ge(max_loaded, M_DMAS * (i + 1))
                if n >= 2:
                    pe.wait_ge(exp_done, NFILL * i + n - 1)
                bank = score_ps[n % 2]
                for at in range(2):
                    kv = 2 * c + (at if s == 2 else s)
                    tile = 2 if s == 2 else at
                    qb = 0 if tile == 0 else 1
                    lo, keys = ((0, K1), (K1, K2), (K1 + K2, K3))[tile]
                    last = mm(bank[0:keys, at * 256:(at + 1) * 256], k_op[:, kv, lo:lo + keys],
                              q_op[:, 2 * kv:2 * kv + 2, qb, :], start=True, stop=True)
                last.then_inc(scores_filled, 1)

            def times_v(i, c, h):
                if h == 0:
                    pe.wait_ge(exp_done, NFILL * i + 3 * c + 3)
                    if c == 0 and past(i, 1):
                        pe.wait_ge(o_normed, 2 * i)
                kv = 2 * c + h
                for pair in range(2):
                    p = 2 * kv + pair
                    cols = slice(pair * 128, pair * 128 + 128)
                    cols2 = slice(256 + pair * 128, 256 + pair * 128 + 128)
                    cols3 = slice(h * 256 + pair * 128, h * 256 + pair * 128 + 128)
                    w, n = D + 1, N_STREAM * (D + 1)
                    o0, o1 = (o_ps[:, at + p * w:at + p * w + n] for at in O_COLS)
                    v = v_sb[:, :, kv:kv + N_STREAM, :].rearrange("p t h d -> p t (h d)")
                    mm(o0, probs[:, c % 2, h, cols], v[:, 0], start=True, stop=True)
                    mm(o1, probs[:, c % 2, h, cols2], v[:, 1], start=True, stop=False)
                    last = mm(o1, probs[0:K3, c % 2, 2, cols3], v[0:K3, 2], start=False, stop=True)
                if h == 1:
                    last.then_inc(pv_done, 1)

            def up_project(j, a):
                last = mm(ffn_ps[:, HID:2 * HID], act_t[:, a, :], up_sb[:, a, :], start=(a == 0), stop=(a == NI1 - 1))
                if a == NI1 - 1:
                    last.then_inc(up_done, 1)

            def transpose_o(i):
                pe.wait_ge(o_normed, 2 * i + 2)
                for qb in range(2):
                    last = nc.tensor.transpose(att_ps[:, qb * 128:(qb + 1) * 128],
                                               o_norm[:, qb].rearrange("p n d -> p (n d)"), ident[:, :])
                last.then_inc(o_transposed, 1)

            def project_o(i):
                pe.wait_ge(o_t_ready, i + 1)
                for h in range(2):
                    last = mm(att_ps[:, HID:2 * HID], o_t[:, h, :], wo_sb[:, h, :], start=(h == 0), stop=(h == 1))
                last.then_inc(wo_done, 1)

            def batch(i, att, mid, late, last):
                j, k = i - 1, i - 2
                for n in range(NFILL + 3):
                    if mid and n < NFILL:
                        scores(j, n)
                    if last and 0 < n <= NI1 - UP_SPLIT:
                        up_project(i - 3, UP_SPLIT + n - 1)
                    if att and n == NFILL:
                        transpose_xn(i)
                    if mid and n // 3 and n % 3:
                        times_v(j, n // 3 - 1, n % 3 - 1)
                if att:
                    project(i)
                if mid:
                    transpose_o(j)
                if late:
                    coefficients(k, 0)
                if mid:
                    project_o(j)
                if late:
                    coefficients(k, 1)
                    coefficients(k, 2)
                if mid:
                    ffn_head(j)
                if late:
                    coefficients(k, 3)
                if mid:
                    query(j, late)
                if late:
                    pe.wait_ge(act_ready, 4 * k + 4)
                    for a in range(UP_QUERY):
                        up_project(k, a)
                if mid:
                    sub_keys(j, late)
                if late:
                    for a in range(UP_QUERY, UP_SIMS):
                        up_project(k, a)
                if mid:
                    for a in range(8):
                        hidden(j, a)
                for n in range(NFILL):
                    if att:
                        max_scores(i, n)
                    if mid and n < 4:
                        hidden(j, 8 + n)
                    if late and n >= 4 and n % 2 and UP_SIMS + (n - 4) // 2 < UP_MAX:
                        up_project(k, UP_SIMS + (n - 4) // 2)
                if att:
                    transpose_max(i)
                if mid:
                    for a in range(12, NI1):
                        hidden(j, a)
                if late:
                    for a in range(UP_MAX, UP_SPLIT):
                        up_project(k, a)

            pe.wait_ge(att_w_loaded, 10 * 16)
            pe.wait_ge(wq_scaled, 1)
            pe.wait_ge(setup_done, 2)
            batch(0, True, False, False, False)
            pe.wait_ge(ffn_w_loaded, 6 * 16)
            batch(1, True, True, False, False)
            pe.wait_ge(up_loaded, 16)
            batch(2, True, True, True, False)
            with pe.Fori(3, B) as i:
                batch(i, True, True, True, True)
            batch(B, False, True, True, True)
            batch(B + 1, False, False, True, True)
            batch(B + 2, False, False, False, True)


def constants():
    bf = np.dtype("bfloat16")
    keys = np.concatenate([np.arange(QB), np.arange(QB), np.arange(T), np.arange(A3_LO, T)])
    window = np.concatenate([np.full(QB, W_SSM), np.full(QB, W_ATT), np.full(K2, W_SSM), np.full(K3, W_ATT)])
    first = np.concatenate([np.zeros(K1), np.full(K2 + K3, QB)])
    delta = first[None, :] + np.arange(QB)[:, None] - keys[None, :]
    krows = np.concatenate([
        np.broadcast_to(keys, (N_ALIBI, KALL)),
        np.where((delta >= 0) & (delta < window[None, :]), 0.0, MASKED),
        np.ones((N_MAX, KALL)),
    ])
    krows = np.broadcast_to(krows[:, None, :], (ROWS - R_ALIBI, NKV, KALL)).astype(bf)
    slope = np.power(np.float32(2.0), (-8.0 * np.arange(NH, dtype=np.float32) / NH).astype(np.float32)).astype(np.float32)
    rest, parts = slope, []
    for _ in range(N_ALIBI):
        parts.append(rest.astype(bf))
        rest = rest - parts[-1].astype(np.float32)
    qrows = np.zeros((R_MAX - R_ALIBI, NP, 2, 2, QB), bf)
    qrows[:N_ALIBI] = np.stack(parts).reshape(N_ALIBI, NP, 1, 2, 1)
    qrows[N_ALIBI:] = np.eye(QB)[:, None, None, None, :]
    qrows = qrows.reshape(R_MAX - R_ALIBI, NP, 2, 2 * QB)
    iota2 = np.broadcast_to(np.arange(NK)[None, :, None], (128, NK, NG)).astype(bf)
    own = np.arange(128)[:, None] // 32 == np.arange(4)[None, :]
    iota1 = np.where(own[:, :, None], np.arange(NI1)[None, None, :], -1)
    iota1 = np.broadcast_to(iota1[..., None], (128, 4, NI1, NG)).astype(bf)
    return {
        "c_ident": np.eye(128, dtype=np.float32), "c_krows": krows, "c_qrows": qrows,
        "c_iota2": iota2, "c_iota1": iota1,
        "c_ranks": np.broadcast_to(np.arange(FK, dtype=np.float32), (128, FK)),
    }


def kernel(x, ctx_2048, g_xattn, g_ffn, L0_xattn_Wq, L0_xattn_Wk, L0_xattn_Wv, L0_xattn_Wsk, L0_xattn_Wsv,
           L0_xattn_Wo, L0_ffn_Wq, L0_ffn_keys, L0_ffn_e_down, L0_ffn_e_up):
    import concourse.bacc as bacc
    from concourse.bass_utils import run_bass_kernel_spmd

    a = np.asarray
    arrays = {
        "x": a(x),
        "ctx_t": a(ctx_2048).transpose(0, 2, 1).reshape(B, KC, 128, T).transpose(0, 2, 1, 3),
        "g": np.broadcast_to(np.concatenate([a(g_xattn), a(g_ffn)]), (128, 2)),
        "wq": a(L0_xattn_Wq).reshape(2 * HID, NP, 2, D).transpose(0, 2, 3, 1).reshape(2 * HID, HID),
        "wk": a(L0_xattn_Wk).reshape(HID, NKV, D).transpose(0, 2, 1).reshape(HID, NKV * D),
        "wv": a(L0_xattn_Wv),
        "wsk": a(L0_xattn_Wsk).reshape(HID, NKV, D).transpose(0, 2, 1).reshape(HID, NKV * D),
        "wsv": a(L0_xattn_Wsv),
        "wo": a(L0_xattn_Wo).reshape(NP, 2, D, HID).transpose(0, 2, 1, 3).reshape(128, 2, HID),
        "fwq": a(L0_ffn_Wq),
        "keys_t": a(L0_ffn_keys).transpose(2, 3, 0, 1).reshape(2 * DK, FH, NK),
        "down_t": a(L0_ffn_e_down).T, "up": a(L0_ffn_e_up),
        **constants(),
    }
    nc = bacc.Bacc("TRN2", target_bir_lowering=False, num_devices=1)
    aps = []
    for name, v in arrays.items():
        arrays[name] = v = np.ascontiguousarray(v)
        aps.append(nc.dram_tensor(name, v.shape, mybir.dt.from_np(v.dtype), kind="ExternalInput").ap())
    aps.append(nc.dram_tensor("out", (B, T, HID), F32, kind="ExternalOutput").ap())
    program(nc, *aps)
    r = run_bass_kernel_spmd(nc, [arrays], core_ids=[0])
    return r.results[0]["out"]
```

```python
from contextlib import ExitStack

import numpy as np

import concourse.bass as bass
from concourse import mybir

F32 = mybir.dt.float32
BF16 = mybir.dt.bfloat16
U32 = mybir.dt.uint32
ALU = mybir.AluOpType
ACT = mybir.ActivationFunctionType
AX_X = mybir.AxisListType.X

B, T, HID = 16, 128, 256
KC = HID // 128
NH, NKV, D = 32, 8, 8
NP = NH // 2
W_SSM, W_ATT = 64, 32
QB = 64
K1, K2, K3 = 128, 128, 96
KALL = K1 + K2 + K3
A3_LO = T - K3
Q_PART = [0, 0, 0, 1, 1, 2]
K_RUNS = [(0, 3), (3, 2), (5, 1)]
R_QK = len(Q_PART) * D
R_ALIBI, N_ALIBI = R_QK, 3
R_MASK = R_ALIBI + N_ALIBI
R_MAX, N_MAX = R_MASK + QB, 2
ROWS = R_MAX + N_MAX
MASKED = -1e30
FH, FK, DK, NK, E = 4, 8, 64, 128, 2048
NI1 = E // NK
NPICK = FH * FK
NG = T // 4
EPS = 1e-5

STORES = 5 * 16
QK_DMAS = (len(Q_PART) + len(K_RUNS)) * 16
M_DMAS = N_MAX * 16
VW = 32
NG4 = 4
NSETS = NKV // NG4
O_COLS = [2 * T, 0]
OW = 4 * NG4 * (D + 1)
UP_QUERY, UP_SIMS, UP_MAX, UP_SPLIT = 2, 4, 7, 12
NFILL = 12


def past(i, n):
    return not isinstance(i, int) or i >= n


def program(nc, x, ctx_t, g, wq, wk, wv, wsk, wsv, wo, fwq, keys_t, down_t, up,
            c_ident, c_pick, c_krows, c_qrows, c_iota2, c_iota1, c_ranks, out):
    st = ExitStack()
    with st:
        def sb(name, shape, dt=F32):
            return st.enter_context(nc.sbuf_tensor(name, shape, dt))

        def ps(name):
            return st.enter_context(nc.psum_tensor(name, [128, 512], F32))

        def sem(name):
            return st.enter_context(nc.semaphore(name))

        wq_sb = sb("wq_sb", [128, 2 * KC, HID])
        wk_sb = sb("wk_sb", [128, 2, KC, NKV * D])
        wv_sb = sb("wv_sb", [128, 2, KC, NKV * D])
        wo_sb = sb("wo_sb", [128, 2, HID])
        fwq_sb = sb("fwq_sb", [128, KC, 2 * FH * DK])
        keys_sb = sb("keys_sb", [128, FH, NK])
        down_sb = sb("down_sb", [128, KC, E])
        up_sb = sb("up_sb", [128, NI1, HID])
        ident = sb("ident", [128, 128])
        iota2 = sb("iota2", [128, NK, NG], BF16)
        iota1 = sb("iota1", [128, 4, NI1, NG], BF16)
        ranks = sb("ranks", [128, FK])
        gates = sb("gates", [128, 2])
        half_neg = sb("half_neg", [128, 1])

        x_in = sb("x_in", [128, HID])
        x_res = sb("x_res", [128, HID])
        ctx_sb = sb("ctx_sb", [128, KC, T])
        stats = sb("stats", [128, 6])
        mv = sb("mv", [128, 2])
        var_eps = sb("var_eps", [128, 1])
        rstd = sb("rstd", [128, 1])
        xn = sb("xn", [128, HID])
        xn_t = sb("xn_t", [128, KC, T])
        qk_parts = sb("qk_parts", [128, 3, 3 * T], BF16)
        qk_rest = sb("qk_rest", [128, 3 * T])
        q_op = sb("q_op", [ROWS, NP, 2, 2 * QB], BF16)
        k_op = sb("k_op", [ROWS, NKV, KALL], BF16)
        v_sb = sb("v_sb", [128, 3, NKV, VW])
        m_neg = sb("m_neg", [128, NP, 2])
        mt_parts = sb("mt_parts", [2 * NP, N_MAX, 128], BF16)
        probs = sb("probs", [128, 4, 3, 512])
        pick = sb("pick", [128, NG4 * (D + 1)])
        o_raw = sb("o_raw", [128, NSETS, 512])
        rden = sb("rden", [128, NSETS, 2, NP // 2])
        o_norm = sb("o_norm", [128, 2, NP, D])
        o_t = sb("o_t", [128, 2, T])
        x2 = sb("x2", [128, HID])
        x2_last = sb("x2_last", [128, HID])

        stats2 = sb("stats2", [128, 6])
        mv2 = sb("mv2", [128, 2])
        var_eps2 = sb("var_eps2", [128, 1])
        rstd2 = sb("rstd2", [128, 1])
        xn2 = sb("xn2", [128, HID])
        xn2_t = sb("xn2_t", [128, KC, T])
        fq_t = sb("fq_t", [128, FH, T])
        sims = sb("sims", [128, 2, FH, NK])
        top_s = sb("top_s", [128, 2, FH, FK])
        top_i = sb("top_i", [128, 2, FH, FK], U32)
        top_if = sb("top_if", [128, 2 * FH, FK])
        pair_s = sb("pair_s", [128, FH, FK, FK])
        fin_s = sb("fin_s", [128, FH, FK])
        fin_i = sb("fin_i", [128, NPICK], U32)
        rank12 = sb("rank12", [128, 2, NPICK], U32)
        hot_r = sb("hot_r", [128, 2 * NPICK, FK])
        val_r = sb("val_r", [128, 2 * NPICK, FK])
        pick_i = sb("pick_i", [128, 2, NPICK])
        beyond = sb("beyond", [128, NPICK])
        picks = sb("picks", [128, 3, NPICK])
        picks_t = sb("picks_t", [128, 3, NG])
        ib = sb("ib", [128, 2, NG], BF16)
        w_parts = sb("w_parts", [128, 3, NG], BF16)
        w_rest = sb("w_rest", [128, NG])
        hot2 = sb("hot2", [128, NK, NG], BF16)
        hot1 = sb("hot1", [128, 4 * NI1, NG], BF16)
        w_hot1 = sb("w_hot1", [128, 3, 4 * NI1, NG], BF16)
        hs = sb("hs", [128, NI1, T])
        act_t = sb("act_t", [128, NI1, T])
        y = sb("y", [128, HID])

        q_scratch = nc.dram_tensor("q_scratch", (3, D, NP, 2 * T), BF16, kind="Internal").ap()
        k_scratch = nc.dram_tensor("k_scratch", (3, D, NKV, KALL), BF16, kind="Internal").ap()

        score_ps = [ps("score_ps0"), ps("score_ps1")]
        o_ps = ps("o_ps")
        att_ps = ps("att_ps")
        h_ps = [ps("h_ps0"), ps("h_ps1")]
        c_ps = ps("c_ps")
        ffn_ps = ps("ffn_ps")
        coef_ps = [h_ps[0], h_ps[1], c_ps, h_ps[0]]

        ident_loaded = sem("ident_loaded")
        wq_loaded = sem("wq_loaded")
        kv_w_loaded = sem("kv_w_loaded")
        att_tables_loaded = sem("att_tables_loaded")
        ffn_w_loaded = sem("ffn_w_loaded")
        ffn_tables_loaded = sem("ffn_tables_loaded")
        up_loaded = sem("up_loaded")
        x_loaded = sem("x_loaded")
        ctx_loaded = sem("ctx_loaded")
        res_loaded = sem("res_loaded")
        parts_stored = sem("parts_stored")
        operands_loaded = sem("operands_loaded")
        max_loaded = sem("max_loaded")
        out_stored = sem("out_stored")
        setup_done = sem("setup_done")
        wq_scaled = sem("wq_scaled")
        gates_ready = sem("gates_ready")
        var_ready = sem("var_ready")
        rstd_ready = sem("rstd_ready")
        xn_ready = sem("xn_ready")
        xn_transposed = sem("xn_transposed")
        xn_t_ready = sem("xn_t_ready")
        qk_projected = sem("qk_projected")
        v_projected = sem("v_projected")
        v_ready = sem("v_ready")
        first_v_ready = sem("first_v_ready")
        hi_ready = sem("hi_ready")
        rest_ready = sem("rest_ready")
        mid_ready = sem("mid_ready")
        parts_ready = sem("parts_ready")
        max_filled = sem("max_filled")
        max_taken = sem("max_taken")
        max_transposed = sem("max_transposed")
        max_split = sem("max_split")
        scores_filled = sem("scores_filled")
        exp_done = sem("exp_done")
        pv_done = sem("pv_done")
        o_raw_ready = sem("o_raw_ready")
        o_filled = sem("o_filled")
        o_normed = sem("o_normed")
        o_transposed = sem("o_transposed")
        o_t_ready = sem("o_t_ready")
        wo_done = sem("wo_done")
        x2_ready = sem("x2_ready")
        var2_ready = sem("var2_ready")
        rstd2_ready = sem("rstd2_ready")
        xn2_ready = sem("xn2_ready")
        xn2_transposed = sem("xn2_transposed")
        xn2_t_ready = sem("xn2_t_ready")
        fq_projected = sem("fq_projected")
        fq_t_ready = sem("fq_t_ready")
        sims_filled = sem("sims_filled")
        sims_ready = sem("sims_ready")
        halves_ready = sem("halves_ready")
        hot2_ready = sem("hot2_ready")
        hot1_made = sem("hot1_made")
        hot1_ready = sem("hot1_ready")
        h_filled = sem("h_filled")
        hs_ready = sem("hs_ready")
        coef_filled = sem("coef_filled")
        act_ready = sem("act_ready")
        up_done = sem("up_done")
        y_ready = sem("y_ready")
        dve_step = sem("dve_step")

        block = st.enter_context(nc.Block())

        @block.sync
        def _(sp):
            def load(dst, src, s):
                sp.dma_start(dst, src).then_inc(s, 16)

            load(x_in[:, :], x[0, :, :], x_loaded)
            load(ident[:, :], c_ident[:, :], ident_loaded)
            load(wq_sb[:, :, :], wq.rearrange("(k p) n -> p k n", p=128), wq_loaded)
            load(ctx_sb[:, :, :], ctx_t[0, :, :, :], ctx_loaded)
            for a, (kk, vv) in enumerate(((wsk, wsv), (wk, wv))):
                load(wk_sb[:, a], kk.rearrange("(k p) n -> p k n", p=128), kv_w_loaded)
                load(wv_sb[:, a], vv.rearrange("(k p) n -> p k n", p=128), kv_w_loaded)
            load(k_op[R_ALIBI:ROWS, :, :], c_krows[:, :, :], att_tables_loaded)
            load(q_op[R_ALIBI:R_MAX, :, :, :], c_qrows[:, :, :, :], att_tables_loaded)
            load(wo_sb[:, :, :], wo[:, :, :], att_tables_loaded)
            load(pick[:, :], c_pick[:, :], att_tables_loaded)
            load(gates[:, :], g[:, :], att_tables_loaded)

            def store_parts(i):
                sp.wait_ge(parts_ready, i + 1)
                load(q_scratch.rearrange("a d n t -> (d n) a t"), qk_parts[:, :, 0:2 * T], parts_stored)
                for a, lo, n, at in ((0, 0, QB, 0), (1, 0, QB, QB), (0, 0, T, K1), (1, A3_LO, K3, K1 + K2)):
                    load(k_scratch[:, :, :, at:at + n].rearrange("a d n t -> (d n) a t"),
                         qk_parts[64 * a:64 * a + 64, :, 2 * T + lo:2 * T + lo + n], parts_stored)

            def operands(i):
                sp.wait_ge(parts_stored, STORES * (i + 1))
                for r, pq in enumerate(Q_PART):
                    load(q_op[D * r:D * r + D, :, :, :].rearrange("r p b t -> r (p b t)"),
                         q_scratch[pq].rearrange("d n t -> d (n t)"), operands_loaded)
                for r, n in K_RUNS:
                    load(k_op[D * r:D * (r + n), :, :].rearrange("r n t -> r (n t)"),
                         k_scratch[0:n].rearrange("a d n t -> (a d) (n t)"), operands_loaded)

            def next_x(i):
                sp.wait_ge(xn_ready, i)
                load(x_in[:, :], x[i, :, :], x_loaded)

            def next_ctx(i):
                sp.wait_ge(v_projected, i)
                load(ctx_sb[:, :, :], ctx_t[i, :, :, :], ctx_loaded)

            def residual(i):
                sp.wait_ge(x2_ready, i)
                load(x_res[:, :], x[i, :, :], res_loaded)

            def maxima(i):
                for part in range(N_MAX):
                    row = R_MAX + part
                    sp.wait_ge(max_split, N_MAX * i + part + 1)
                    load(q_op[row:row + 1, :, :, :].rearrange("r p b t -> r (p b) t"), mt_parts[:, part, :], max_loaded)

            def store(j):
                sp.wait_ge(y_ready, j + 1)
                sp.dma_start(out[j, :, :], y[:, :]).then_inc(out_stored, 16)

            store_parts(0)
            next_x(1)
            operands(0)
            next_ctx(1)
            load(x_res[:, :], x[0, :, :], res_loaded)
            load(fwq_sb[:, :, :], fwq.rearrange("(k p) n -> p k n", p=128), ffn_w_loaded)
            load(keys_sb[:, :, :], keys_t[:, :, :], ffn_w_loaded)
            load(down_sb[:, :, :], down_t.rearrange("(k p) n -> p k n", p=128), ffn_w_loaded)
            maxima(0)
            load(iota2[:, :, :], c_iota2[:, :, :], ffn_tables_loaded)
            load(iota1[:, :, :, :], c_iota1[:, :, :, :], ffn_tables_loaded)
            load(ranks[:, :], c_ranks[:, :], ffn_tables_loaded)
            load(up_sb[:, :, :], up.rearrange("(a p) n -> p a n", p=128), up_loaded)
            for i in (1, 2):
                store_parts(i)
                next_x(i + 1)
                operands(i)
                next_ctx(i + 1)
                residual(i)
                maxima(i)
            with sp.Fori(3, B - 1) as i:
                store(i - 3)
                store_parts(i)
                sp.wait_ge(out_stored, 16 * (i - 2))
                load(x_in[:, :], x[i + 1, :, :], x_loaded)
                operands(i)
                next_ctx(i + 1)
                residual(i)
                maxima(i)
            store(B - 4)
            store_parts(B - 1)
            operands(B - 1)
            residual(B - 1)
            maxima(B - 1)
            for j in range(B - 3, B):
                store(j)
            sp.wait_ge(out_stored, 16 * B)

        @block.gpsimd
        def _(pool):
            pool.memset(half_neg[:, :], -0.5).then_inc(setup_done, 1)
            pool.memset(v_sb[:, :, :, :], 1.0).then_inc(setup_done, 1)
            pool.wait_ge(setup_done, 1)

            def norm1(i):
                pool.wait_ge(var_ready, i + 1)
                pool.tensor_tensor(rstd[:, :], var_eps[:, :], half_neg[:, :], ALU.pow).then_inc(rstd_ready, 1)

            def norm2(i):
                pool.wait_ge(var2_ready, i + 1)
                pool.tensor_tensor(rstd2[:, :], var_eps2[:, :], half_neg[:, :], ALU.pow).then_inc(rstd2_ready, 1)

            def weights(k):
                pool.wait_ge(hot1_made, k + 1)
                pool.tensor_tensor(w_hot1[:, 2], hot1[:, :, :],
                                   w_parts[:, 2, :].unsqueeze(1).broadcast_to([128, 4 * NI1, NG]),
                                   ALU.mult).then_inc(hot1_ready, 1)

            norm1(0)
            norm1(1)
            norm2(0)
            norm1(2)
            with pool.Fori(2, B - 1) as i:
                weights(i - 2)
                norm2(i - 1)
                norm1(i + 1)
            weights(B - 3)
            norm2(B - 2)
            weights(B - 2)
            norm2(B - 1)
            weights(B - 1)

        @block.scalar
        def _(act):
            act.wait_ge(wq_loaded, 16)
            nc.scalar.mul(wq_sb[:, :, :], wq_sb[:, :, :], float(D) ** -0.5).then_inc(wq_scaled, 1)
            act.wait_ge(setup_done, 2)

            def att_head(i):
                act.wait_ge(xn_transposed, i + 1)
                nc.scalar.copy(xn_t[:, :, :], att_ps[:, 0:KC * T].rearrange("p (k t) -> p k t", t=T)).then_inc(xn_t_ready, 1)

            def att_parts(i, mid):
                act.wait_ge(qk_projected, i + 1)
                act.wait_ge(parts_stored, STORES * i)
                blocks = "p (h b q) -> p b h q"
                nc.scalar.copy(qk_parts[:, 0, 0:2 * T].rearrange("p (b h q) -> p b h q", b=2, h=2),
                               score_ps[0][:, 0:2 * T].rearrange(blocks, h=2, b=2))
                nc.scalar.copy(qk_parts[:, 0, 2 * T:3 * T], score_ps[0][:, 2 * T:3 * T]).then_inc(hi_ready, 1)
                if mid:
                    att_tail(i - 1)
                act.wait_ge(rest_ready, i + 1)
                nc.scalar.copy(qk_parts[:, 1, :], qk_rest[:, :]).then_inc(mid_ready, 1)
                act.wait_ge(v_projected, i + 1)
                v = score_ps[1][:, 0:3 * NKV * D].rearrange("p (n h d) -> p n h d", n=3, d=D)
                nc.scalar.copy(v_sb[:, 1, 0:NKV, 0:D], v[:, 1])
                nc.scalar.copy(v_sb[0:K3, 2, 0:NKV, 0:D], v[0:K3, 2]).then_inc(v_ready, 1)

            def ffn_head(j):
                act.wait_ge(xn2_transposed, j + 1)
                nc.scalar.copy(xn2_t[:, :, :], ffn_ps[:, 0:KC * T].rearrange("p (k t) -> p k t", t=T)).then_inc(xn2_t_ready, 1)

            def ffn_sims(j):
                act.wait_ge(fq_projected, j + 1)
                nc.scalar.copy(fq_t[:, :, :], c_ps[:, :].rearrange("p (h t) -> p h t", t=T)).then_inc(fq_t_ready, 1)
                act.wait_ge(sims_filled, j + 1)
                for half in range(2):
                    nc.scalar.copy(sims[:, half], h_ps[half][:, :].rearrange("p (h n) -> p h n", n=NK)).then_inc(sims_ready, 1)

            def silus(j):
                for c in range(4):
                    act.wait_ge(h_filled, 4 * j + c + 1)
                    nc.scalar.activation(hs[:, 4 * c:4 * c + 4, :].rearrange("p a t -> p (a t)"), h_ps[c % 2][:, :],
                                         ACT.Silu).then_inc(hs_ready, 1)

            def outputs_copy(i, s):
                act.wait_ge(pv_done, 2 * i + s + 1)
                nc.scalar.copy(o_raw[:, s, :], o_ps[:, :]).then_inc(o_raw_ready, 1)

            def exps(i, att):
                for n in range(NFILL):
                    if n == 0 and past(i, 1):
                        act.wait_ge(pv_done, 2 * i)
                    c, s = n // 3, n % 3
                    keys = K3 if s == 2 else 128
                    act.wait_ge(scores_filled, NFILL * i + n + 1)
                    nc.scalar.activation(probs[0:keys, c, s, :], score_ps[n % 2][0:keys, :], ACT.Exp).then_inc(exp_done, 1)
                    if att and n == 6:
                        att_head(i + 1)
                    if n == 8:
                        outputs_copy(i, 0)

            def att_tail(i):
                act.wait_ge(o_transposed, i + 1)
                src = att_ps[:, 0:2 * 128].rearrange("p (b h q) -> p h b q", b=2, h=2)
                nc.scalar.copy(o_t[:, :, :].rearrange("p h (b q) -> p h b q", b=2), src).then_inc(o_t_ready, 1)

            def batch(i, att, mid):
                if mid:
                    exps(i - 1, att)
                    outputs_copy(i - 1, 1)
                elif att:
                    att_head(i)
                if att:
                    att_parts(i, mid)
                if mid:
                    if not att:
                        att_tail(i - 1)
                    ffn_head(i - 1)
                    ffn_sims(i - 1)
                    silus(i - 1)

            batch(0, True, False)
            act.wait_ge(att_tables_loaded, 5 * 16)
            nc.scalar.activation(gates[:, :], gates[:, :], ACT.Tanh).then_inc(gates_ready, 1)
            batch(1, True, True)
            with act.Fori(2, B) as i:
                batch(i, True, True)
            batch(B, False, True)

        @block.vector
        def _(dve):
            v = nc.vector
            steps = {"n": 0}

            def link(ins):
                steps["n"] += 1
                ins.then_inc(dve_step, 1)
                dve.wait_ge(dve_step, steps["n"])

            def restart():
                dve.sem_clear(dve_step)
                steps["n"] = 0

            def norm_stats(src, stats, mv, var_eps, var_sem):
                link(v.bn_stats(stats[:, :], src[:, :]))
                link(v.bn_aggr(mv[:, :], stats[:, :]))
                v.tensor_scalar_add(var_eps[:, :], mv[:, 1:2], EPS).then_inc(var_sem, 1)

            def att_norm(i):
                dve.wait_ge(x_loaded, 16 * i + 16)
                norm_stats(x_in, stats, mv, var_eps, var_ready)
                dve.wait_ge(rstd_ready, i + 1)
                if past(i, 1):
                    dve.wait_ge(xn_transposed, i)
                norm_apply(x_in, mv, rstd, xn, xn_ready)

            def norm_apply(src, mv, rstd, xn, sem):
                v.tensor_scalar(xn[:, :], src[:, :], mv[:, 0:1], rstd[:, 0:1], ALU.subtract, ALU.mult).then_inc(sem, 1)

            def att_parts(i):
                dve.wait_ge(hi_ready, i + 1)
                blocks, put = "p (h b q) -> p b h q", "p (b h q) -> p b h q"
                v.tensor_tensor(qk_rest[:, 0:2 * T].rearrange(put, b=2, h=2), score_ps[0][:, 0:2 * T].rearrange(blocks, h=2, b=2),
                                qk_parts[:, 0, 0:2 * T].rearrange(put, b=2, h=2), ALU.subtract)
                v.tensor_tensor(qk_rest[:, 2 * T:3 * T], score_ps[0][:, 2 * T:3 * T], qk_parts[:, 0, 2 * T:3 * T],
                                ALU.subtract).then_inc(rest_ready, 1)
                dve.wait_ge(mid_ready, i + 1)
                v.tensor_tensor(qk_parts[:, 2, :], qk_rest[:, :], qk_parts[:, 1, :], ALU.subtract).then_inc(parts_ready, 1)

            def first_v(upper):
                r = slice(64 * upper, 64 * upper + 64)
                src = score_ps[1][r, (1 - upper) * NKV * D:(2 - upper) * NKV * D]
                v.tensor_copy(v_sb[r, 0, 0:NKV, 0:D], src.rearrange("p (h d) -> p h d", d=D)).then_inc(first_v_ready, 1)

            def top_halves(j, att):
                for half in range(2):
                    dve.wait_ge(sims_ready, 2 * j + half + 1)
                    if att:
                        first_v(half)
                    for h in range(FH):
                        last = v.max(top_s[:, half, h], sims[:, half, h])
                last.then_inc(halves_ready, 1)

            def top(j):
                dve.wait_ge(halves_ready, j + 1)
                link(v.tensor_tensor(pair_s[:, :, :, :], top_s[:, 0].unsqueeze(3).broadcast_to([128, FH, FK, FK]),
                                     top_s[:, 1].unsqueeze(2).broadcast_to([128, FH, FK, FK]), ALU.add))
                for half in range(2):
                    for h in range(FH):
                        last = v.max_index(top_i[:, half, h], top_s[:, half, h], sims[:, half, h])
                link(last)
                v.tensor_copy(top_if[:, :, :], top_i[:, :, :, :].rearrange("p a h k -> p (a h) k"))
                for h in range(FH):
                    last = v.max(fin_s[:, h], pair_s[:, h].rearrange("p a b -> p (a b)"))
                link(last)
                for h in range(FH):
                    last = v.max_index(fin_i[:, h * FK:(h + 1) * FK], fin_s[:, h], pair_s[:, h].rearrange("p a b -> p (a b)"))
                link(last)
                v.tensor_scalar(rank12[:, 0, :], fin_i[:, :], 3, None, ALU.logical_shift_right)
                link(v.tensor_scalar(rank12[:, 1, :], fin_i[:, :], FK - 1, None, ALU.bitwise_and))
                link(v.tensor_tensor(hot_r[:, :, :],
                                     rank12[:, :, :].rearrange("p a n -> p (a n)").unsqueeze(2).broadcast_to([128, 2 * NPICK, FK]),
                                     ranks[:, :].unsqueeze(1).broadcast_to([128, 2 * NPICK, FK]), ALU.is_equal))
                link(v.tensor_tensor(val_r[:, :, :].rearrange("p (a k) r -> p a k r", k=FK),
                                     hot_r[:, :, :].rearrange("p (a k) r -> p a k r", k=FK),
                                     top_if[:, :, :].unsqueeze(2).broadcast_to([128, 2 * FH, FK, FK]), ALU.mult))
                link(v.tensor_reduce(pick_i[:, :, :].rearrange("p a n -> p (a n)"), val_r[:, :, :], AX_X, ALU.add))
                v.tensor_scalar(beyond[:, :], pick_i[:, 0, :], float(NI1), float(NK - 1), ALU.is_ge, ALU.mult)
                v.tensor_scalar(picks[:, 0, :], pick_i[:, 0, :], float(NI1 - 1), None, ALU.min)
                link(v.tensor_scalar(picks[:, 2, :], fin_s[:, :, :].rearrange("p h k -> p (h k)"), 0.0, None, ALU.max))
                link(v.tensor_tensor(picks[:, 1, :], pick_i[:, 1, :], beyond[:, :], ALU.max))
                link(v.transpose(picks_t[:, :, :].rearrange("p a g -> p (a g)"), picks[:, :, :].rearrange("p a n -> p (a n)")))
                v.tensor_copy(ib[:, :, :], picks_t[:, 0:2, :])
                link(v.tensor_copy(w_parts[:, 0, :], picks_t[:, 2, :]))
                link(v.tensor_tensor(w_rest[:, :], picks_t[:, 2, :], w_parts[:, 0, :], ALU.subtract))
                link(v.tensor_copy(w_parts[:, 1, :], w_rest[:, :]))
                link(v.tensor_tensor(w_parts[:, 2, :], w_rest[:, :], w_parts[:, 1, :], ALU.subtract))

            def one_hots(j):
                v.tensor_tensor(hot1[:, :, :], iota1[:, :, :, :].rearrange("p j a g -> p (j a) g"),
                                ib[:, 0, :].unsqueeze(1).broadcast_to([128, 4 * NI1, NG]), ALU.is_equal).then_inc(hot1_made, 1)
                v.tensor_tensor(hot2[:, :, :], iota2[:, :, :], ib[:, 1, :].unsqueeze(1).broadcast_to([128, NK, NG]),
                                ALU.is_equal).then_inc(hot2_ready, 1)
                dve.wait_ge(hot1_made, j + 1)
                for part in range(2):
                    v.tensor_tensor(w_hot1[:, part], hot1[:, :, :],
                                    w_parts[:, part, :].unsqueeze(1).broadcast_to([128, 4 * NI1, NG]), ALU.mult).then_inc(hot1_ready, 1)

            def maxima(i, n):
                dve.wait_ge(max_filled, NFILL * i + n + 1)
                bank = score_ps[n % 2]
                if n < 4:
                    dst, src = m_neg[:, 4 * n:4 * n + 4, 0], bank[:, :].rearrange("p (a k) -> p a k", k=K1)
                else:
                    m = n - 4
                    dst = m_neg[:, 2 * m:2 * m + 2, 1]
                    src = bank[:, 0:2 * (K2 + K3)].rearrange("p (a k) -> p a k", k=K2 + K3)
                v.tensor_reduce(dst, src, AX_X, ALU.max, negate=True).then_inc(max_taken, 1)

            def max_parts(i):
                dve.wait_ge(max_transposed, i + 1)
                dve.wait_ge(max_loaded, M_DMAS * i)
                mt = att_ps[0:2 * NP, 2 * T:3 * T]
                v.tensor_copy(mt_parts[:, 0, :], mt).then_inc(max_split, 1)
                dve.wait_ge(max_split, N_MAX * i + 1)
                v.tensor_tensor(mt_parts[:, 1, :], mt, mt_parts[:, 0, :], ALU.subtract).then_inc(max_split, 1)

            def activations(k, c):
                dve.wait_ge(coef_filled, 4 * k + c + 1)
                if c == 0:
                    dve.wait_ge(hs_ready, 4 * k + 4)
                gs = slice(c * 8, c * 8 + 8)
                view = "p a (j g) -> p g j a"
                v.tensor_tensor(act_t[:, :, :].rearrange(view, j=4)[:, gs],
                                coef_ps[c][:, :].rearrange("p (g j a) -> p g j a", j=4, a=NI1),
                                hs[:, :, :].rearrange(view, j=4)[:, gs], ALU.mult).then_inc(act_ready, 1)

            def ffn_tail(k):
                dve.wait_ge(up_done, k + 1)
                v.scalar_tensor_tensor(out=y[:, :], in0=ffn_ps[:, HID:2 * HID], scalar=gates[:, 1:2], in1=x2_last[:, :],
                                       op0=ALU.mult, op1=ALU.add).then_inc(y_ready, 1)

            def att_normalise(i):
                dve.wait_ge(o_filled, 2 * i + 2)
                o = [att_ps[:, at:at + OW].rearrange("p (b n d) -> p b n d", b=2, d=D + 1) for at in O_COLS]
                v.reciprocal(rden[:, 0], o[0][:, :, :, D])
                link(v.reciprocal(rden[:, 1], o[1][:, :, :, D]))
                for s in range(NSETS):
                    v.tensor_tensor(o_norm[:, :, 8 * s:8 * s + 8], o[s][:, :, :, 0:D],
                                    rden[:, s].unsqueeze(3).broadcast_to([128, 2, NP // 2, D]), ALU.mult).then_inc(o_normed, 1)

            def att_residual(i):
                dve.wait_ge(wo_done, i + 1)
                dve.wait_ge(res_loaded, 16 * i + 16)
                v.scalar_tensor_tensor(out=x2[:, :], in0=att_ps[:, HID:2 * HID], scalar=gates[:, 0:1], in1=x_res[:, :],
                                       op0=ALU.mult, op1=ALU.add).then_inc(x2_ready, 1)

            def batch(i, att, mid, late, last, following=False):
                j, k = i - 1, i - 2
                if late:
                    top(k)
                    one_hots(k)
                if mid:
                    att_normalise(j)
                if last:
                    if not att:
                        dve.wait_ge(out_stored, 16 * (i - 3))
                    ffn_tail(i - 3)
                    dve.wait_ge(y_ready, i - 2)
                if late:
                    link(v.tensor_copy(x2_last[:, :], x2[:, :]))
                if att:
                    att_parts(i)
                if mid:
                    att_residual(j)
                    dve.wait_ge(x2_ready, j + 1)
                    norm_stats(x2, stats2, mv2, var_eps2, var2_ready)
                if late:
                    activations(k, 0)
                if mid:
                    dve.wait_ge(rstd2_ready, j + 1)
                    if late:
                        dve.wait_ge(xn2_transposed, j)
                    norm_apply(x2, mv2, rstd2, xn2, xn2_ready)
                if late:
                    for c in range(1, 4):
                        activations(k, c)
                if following:
                    att_norm(i + 1)
                if att:
                    dve.wait_ge(v_ready, i + 1)
                if att and not mid:
                    first_v(0)
                    first_v(1)
                if mid:
                    top_halves(j, att)
                if att:
                    for n in range(NFILL):
                        maxima(i, n)
                    max_parts(i)

            att_norm(0)
            batch(0, True, False, False, False, True)
            restart()
            dve.wait_ge(gates_ready, 1)
            batch(1, True, True, False, False, True)
            restart()
            dve.wait_ge(ffn_tables_loaded, 3 * 16)
            batch(2, True, True, True, False, True)
            with dve.Fori(3, B - 1) as i:
                restart()
                batch(i, True, True, True, True, True)
            restart()
            batch(B - 1, True, True, True, True)
            batch(B, False, True, True, True)
            batch(B + 1, False, False, True, True)
            batch(B + 2, False, False, False, True)

        @block.tensor
        def _(pe):
            mm = nc.tensor.matmul

            def transpose_xn(i):
                if not past(i, 1):
                    pe.wait_ge(ident_loaded, 16)
                pe.wait_ge(xn_ready, i + 1)
                if past(i, 2):
                    pe.wait_ge(o_t_ready, i - 1)
                for k in range(KC):
                    last = nc.tensor.transpose(att_ps[:, k * T:(k + 1) * T], xn[:, k * 128:(k + 1) * 128], ident[:, :])
                last.then_inc(xn_transposed, 1)

            def ffn_head(j):
                pe.wait_ge(xn2_ready, j + 1)
                for k in range(KC):
                    last = nc.tensor.transpose(ffn_ps[:, k * T:(k + 1) * T], xn2[:, k * 128:(k + 1) * 128], ident[:, :])
                last.then_inc(xn2_transposed, 1)

            def project_first(i):
                if not past(i, 1):
                    pe.wait_ge(wq_scaled, 1)
                    pe.wait_ge(kv_w_loaded, 4 * 16)
                pe.wait_ge(ctx_loaded, 16 * i + 16)
                pe.wait_ge(xn_t_ready, i + 1)
                if past(i, 1):
                    pe.wait_ge(exp_done, NFILL * i)
                project_q(0)

            src = [ctx_sb, xn_t]

            def project_q(c):
                for k in range(2 * KC):
                    mm(score_ps[0][:, c * T:(c + 1) * T], wq_sb[:, k, c * 128:(c + 1) * 128],
                       src[k // KC][:, k % KC, :], start=(k == 0), stop=(k == 2 * KC - 1))

            def project_rest():
                project_q(1)
                for a in range(2):
                    for k in range(KC):
                        last = mm(score_ps[0][64 * a:64 * a + 64, 2 * T:3 * T], wk_sb[:, a, k, :], src[a][:, k, :],
                                  start=(k == 0), stop=(k == KC - 1))
                last.then_inc(qk_projected, 1)

            def project_v():
                n = NKV * D
                for slot, a, rows, lo, m in ((0, 1, 64, 0, 64), (1, 0, 0, 0, T), (2, 1, 0, A3_LO, K3)):
                    for k in range(KC):
                        last = mm(score_ps[1][rows:rows + m, slot * n:(slot + 1) * n], src[a][:, k, lo:lo + m],
                                  wv_sb[:, a, k, :], start=(k == 0), stop=(k == KC - 1))
                last.then_inc(v_projected, 1)

            def query(j, late):
                pe.wait_ge(xn2_t_ready, j + 1)
                if late:
                    pe.wait_ge(act_ready, 4 * j - 1)
                for h in range(FH):
                    for k in range(KC):
                        last = mm(c_ps[:, h * T:(h + 1) * T], fwq_sb[:, k, h * 128:(h + 1) * 128], xn2_t[:, k, :],
                                  start=(k == 0), stop=(k == KC - 1))
                last.then_inc(fq_projected, 1)

            def sub_keys(j, late):
                pe.wait_ge(fq_t_ready, j + 1)
                if late:
                    pe.wait_ge(act_ready, 4 * j)
                for h in range(FH):
                    for half in range(2):
                        r = slice(64 * half, 64 * half + 64)
                        last = mm(h_ps[half][:, h * NK:(h + 1) * NK], fq_t[r, h, :], keys_sb[r, h, :], start=True, stop=True)
                last.then_inc(sims_filled, 1)

            def hidden(j, a):
                c = a // 4
                if a == 4 * c:
                    if c < 2:
                        pe.wait_ge(sims_ready, 2 * j + c + 1)
                    else:
                        pe.wait_ge(hs_ready, 4 * j + c - 1)
                for k in range(KC):
                    last = mm(h_ps[c % 2][:, a % 4 * T:(a % 4 + 1) * T], down_sb[:, k, a * NK:(a + 1) * NK],
                              xn2_t[:, k, :], start=(k == 0), stop=(k == KC - 1))
                if a == 4 * c + 3:
                    last.then_inc(h_filled, 1)

            def max_scores(i, n):
                if n == 0:
                    if not past(i, 1):
                        pe.wait_ge(att_tables_loaded, 5 * 16)
                    pe.wait_ge(operands_loaded, QK_DMAS * (i + 1))
                    pe.wait_ge(rest_ready, i + 1)
                elif n == 1:
                    pe.wait_ge(first_v_ready, 2 * i + 2)
                else:
                    pe.wait_ge(max_taken, NFILL * i + n - 1)
                qb = 0 if n < 4 else 1
                pairs = range(4 * n, 4 * n + 4) if n < 4 else range(2 * (n - 4), 2 * (n - 4) + 2)
                lo, width = (0, K1) if qb == 0 else (K1, K2 + K3)
                for at, p in enumerate(pairs):
                    last = mm(score_ps[n % 2][:, at * width:(at + 1) * width],
                              q_op[0:R_MAX, p, qb, :],
                              k_op[0:R_MAX, p // 2, lo:lo + width], start=True, stop=True)
                last.then_inc(max_filled, 1)

            def transpose_max(i):
                pe.wait_ge(max_taken, NFILL * i + NFILL)
                if past(i, 1):
                    pe.wait_ge(x2_ready, i)
                nc.tensor.transpose(att_ps[0:2 * NP, 2 * T:3 * T], m_neg[:, :, :].rearrange("p n b -> p (n b)"),
                                    ident[:, :]).then_inc(max_transposed, 1)

            def coefficients(j, c):
                if c == 0:
                    pe.wait_ge(hot2_ready, j + 1)
                    pe.wait_ge(hot1_ready, 3 * j + 3)
                    pe.wait_ge(hs_ready, 4 * j + 4)
                elif c == 3:
                    pe.wait_ge(act_ready, 4 * j + 1)
                for gi in range(8):
                    gg = 8 * c + gi
                    for part in range(3):
                        last = mm(coef_ps[c][:, gi * 64:(gi + 1) * 64], hot2[:, :, gg], w_hot1[:, part, :, gg],
                                  start=(part == 0), stop=(part == 2))
                last.then_inc(coef_filled, 1)

            def scores(i, n):
                c, s = n // 3, n % 3
                if n == 0:
                    pe.wait_ge(max_loaded, M_DMAS * (i + 1))
                if n >= 2:
                    pe.wait_ge(exp_done, NFILL * i + n - 1)
                bank = score_ps[n % 2]
                for at in range(2):
                    kv = 2 * c + (at if s == 2 else s)
                    tile = 2 if s == 2 else at
                    qb = 0 if tile == 0 else 1
                    lo, keys = ((0, K1), (K1, K2), (K1 + K2, K3))[tile]
                    last = mm(bank[0:keys, at * 256:(at + 1) * 256], k_op[:, kv, lo:lo + keys],
                              q_op[:, 2 * kv:2 * kv + 2, qb, :], start=True, stop=True)
                last.then_inc(scores_filled, 1)

            def times_v(i, s, tile):
                if tile == 2:
                    pe.wait_ge(exp_done, NFILL * i + 6 * s + 6)
                elif tile == 0:
                    pe.wait_ge(exp_done, NFILL * i + 6 * s + 5)
                    if s or past(i, 1):
                        pe.wait_ge(o_raw_ready, 2 * i + s)
                keys, cols = K3 if tile == 2 else 128, slice(256 * min(tile, 1), 256 * min(tile, 1) + 256)
                for g in range(NG4):
                    kv = NG4 * s + g
                    c, h = kv // 2, kv % 2
                    p = probs[0:keys, c, 2, h * 256:h * 256 + 256] if tile == 2 else probs[:, c, h, tile * 256:tile * 256 + 256]
                    last = mm(o_ps[VW * g:VW * g + VW, cols], v_sb[0:keys, tile, kv, :], p,
                              start=(tile < 2), stop=(tile != 1))
                if tile == 2:
                    last.then_inc(pv_done, 1)

            def outputs(i, s):
                pe.wait_ge(o_raw_ready, 2 * i + s + 1)
                n = NG4 * (D + 1)
                for be in range(4):
                    at = O_COLS[s] + be * n
                    last = mm(att_ps[:, at:at + n], o_raw[:, s, be * 128:be * 128 + 128], pick[:, :], start=True, stop=True)
                last.then_inc(o_filled, 1)

            def up_project(j, a):
                last = mm(ffn_ps[:, HID:2 * HID], act_t[:, a, :], up_sb[:, a, :], start=(a == 0), stop=(a == NI1 - 1))
                if a == NI1 - 1:
                    last.then_inc(up_done, 1)

            def transpose_o(i):
                pe.wait_ge(o_normed, 2 * i + 2)
                for qb in range(2):
                    last = nc.tensor.transpose(att_ps[:, qb * 128:(qb + 1) * 128],
                                               o_norm[:, qb].rearrange("p n d -> p (n d)"), ident[:, :])
                last.then_inc(o_transposed, 1)

            def project_o(i):
                pe.wait_ge(o_t_ready, i + 1)
                for h in range(2):
                    last = mm(att_ps[:, HID:2 * HID], o_t[:, h, :], wo_sb[:, h, :], start=(h == 0), stop=(h == 1))
                last.then_inc(wo_done, 1)

            def batch(i, att, mid, late, last):
                j, k = i - 1, i - 2
                for n in range(NFILL):
                    if mid:
                        scores(j, n)
                    if last and 0 < n <= NI1 - UP_SPLIT:
                        up_project(i - 3, UP_SPLIT + n - 1)
                    if att and n == 5:
                        transpose_xn(i)
                    if mid and 6 <= n < 9:
                        times_v(j, 0, n - 6)
                    if mid and n == 10:
                        if att:
                            pe.wait_ge(xn_t_ready, i + 1)
                        outputs(j, 0)
                if mid:
                    for tile in range(3):
                        times_v(j, 1, tile)
                if att:
                    project_first(i)
                if mid:
                    outputs(j, 1)
                if att:
                    project_rest()
                if mid:
                    transpose_o(j)
                if late:
                    coefficients(k, 0)
                if mid:
                    project_o(j)
                if late:
                    coefficients(k, 1)
                    coefficients(k, 2)
                if att:
                    project_v()
                if mid:
                    ffn_head(j)
                if late:
                    coefficients(k, 3)
                if mid:
                    query(j, late)
                if late:
                    pe.wait_ge(act_ready, 4 * k + 4)
                    for a in range(UP_QUERY):
                        up_project(k, a)
                if mid:
                    sub_keys(j, late)
                if late:
                    for a in range(UP_QUERY, UP_SIMS):
                        up_project(k, a)
                if mid:
                    for a in range(4):
                        hidden(j, a)
                for n in range(NFILL):
                    if att:
                        max_scores(i, n)
                    if mid and n < 8:
                        hidden(j, 4 + n)
                    if late and NFILL - n <= UP_MAX - UP_SIMS:
                        up_project(k, UP_MAX + n - NFILL)
                if att:
                    transpose_max(i)
                if mid:
                    for a in range(12, NI1):
                        hidden(j, a)
                if late:
                    for a in range(UP_MAX, UP_SPLIT):
                        up_project(k, a)

            batch(0, True, False, False, False)
            pe.wait_ge(setup_done, 2)
            pe.wait_ge(ffn_w_loaded, 3 * 16)
            batch(1, True, True, False, False)
            pe.wait_ge(up_loaded, 16)
            batch(2, True, True, True, False)
            with pe.Fori(3, B) as i:
                batch(i, True, True, True, True)
            batch(B, False, True, True, True)
            batch(B + 1, False, False, True, True)
            batch(B + 2, False, False, False, True)


def constants():
    bf = np.dtype("bfloat16")
    keys = np.concatenate([np.arange(QB), np.arange(QB), np.arange(T), np.arange(A3_LO, T)])
    window = np.concatenate([np.full(QB, W_SSM), np.full(QB, W_ATT), np.full(K2, W_SSM), np.full(K3, W_ATT)])
    first = np.concatenate([np.zeros(K1), np.full(K2 + K3, QB)])
    delta = first[None, :] + np.arange(QB)[:, None] - keys[None, :]
    krows = np.concatenate([
        np.broadcast_to(keys, (N_ALIBI, KALL)),
        np.where((delta >= 0) & (delta < window[None, :]), 0.0, MASKED),
        np.ones((N_MAX, KALL)),
    ])
    krows = np.broadcast_to(krows[:, None, :], (ROWS - R_ALIBI, NKV, KALL)).astype(bf)
    slope = np.power(np.float32(2.0), (-8.0 * np.arange(NH, dtype=np.float32) / NH).astype(np.float32)).astype(np.float32)
    rest, parts = slope, []
    for _ in range(N_ALIBI):
        parts.append(rest.astype(bf))
        rest = rest - parts[-1].astype(np.float32)
    qrows = np.zeros((R_MAX - R_ALIBI, NP, 2, 2, QB), bf)
    qrows[:N_ALIBI] = np.stack(parts).reshape(N_ALIBI, NP, 1, 2, 1)
    qrows[N_ALIBI:] = np.eye(QB)[:, None, None, None, :]
    qrows = qrows.reshape(R_MAX - R_ALIBI, NP, 2, 2 * QB)
    iota2 = np.broadcast_to(np.arange(NK)[None, :, None], (128, NK, NG)).astype(bf)
    own = np.arange(128)[:, None] // 32 == np.arange(4)[None, :]
    iota1 = np.where(own[:, :, None], np.arange(NI1)[None, None, :], -1)
    iota1 = np.broadcast_to(iota1[..., None], (128, 4, NI1, NG)).astype(bf)
    return {
        "c_ident": np.eye(128, dtype=np.float32),
        "c_pick": np.eye(128, dtype=np.float32).reshape(128, NG4, VW)[:, :, :D + 1].reshape(128, NG4 * (D + 1)),
        "c_krows": krows, "c_qrows": qrows,
        "c_iota2": iota2, "c_iota1": iota1,
        "c_ranks": np.broadcast_to(np.arange(FK, dtype=np.float32), (128, FK)),
    }


def kernel(x, ctx_2048, g_xattn, g_ffn, L0_xattn_Wq, L0_xattn_Wk, L0_xattn_Wv, L0_xattn_Wsk, L0_xattn_Wsv,
           L0_xattn_Wo, L0_ffn_Wq, L0_ffn_keys, L0_ffn_e_down, L0_ffn_e_up):
    import concourse.bacc as bacc
    from concourse.bass_utils import run_bass_kernel_spmd

    a = np.asarray
    arrays = {
        "x": a(x),
        "ctx_t": a(ctx_2048).transpose(0, 2, 1).reshape(B, KC, 128, T).transpose(0, 2, 1, 3),
        "g": np.broadcast_to(np.concatenate([a(g_xattn), a(g_ffn)]), (128, 2)),
        "wq": a(L0_xattn_Wq).reshape(2 * HID, NP, 2, D).transpose(0, 2, 3, 1).reshape(2 * HID, HID),
        "wk": a(L0_xattn_Wk).reshape(HID, NKV, D).transpose(0, 2, 1).reshape(HID, NKV * D),
        "wv": a(L0_xattn_Wv),
        "wsk": a(L0_xattn_Wsk).reshape(HID, NKV, D).transpose(0, 2, 1).reshape(HID, NKV * D),
        "wsv": a(L0_xattn_Wsv),
        "wo": a(L0_xattn_Wo).reshape(NSETS, NG4, 2, 2, D, HID).transpose(0, 2, 1, 4, 3, 5).reshape(128, 2, HID),
        "fwq": a(L0_ffn_Wq),
        "keys_t": a(L0_ffn_keys).transpose(2, 3, 0, 1).reshape(2 * DK, FH, NK),
        "down_t": a(L0_ffn_e_down).T, "up": a(L0_ffn_e_up),
        **constants(),
    }
    nc = bacc.Bacc("TRN2", target_bir_lowering=False, num_devices=1)
    aps = []
    for name, v in arrays.items():
        arrays[name] = v = np.ascontiguousarray(v)
        aps.append(nc.dram_tensor(name, v.shape, mybir.dt.from_np(v.dtype), kind="ExternalInput").ap())
    aps.append(nc.dram_tensor("out", (B, T, HID), F32, kind="ExternalOutput").ap())
    program(nc, *aps)
    r = run_bass_kernel_spmd(nc, [arrays], core_ids=[0])
    return r.results[0]["out"]
```
